# Optimizing a Trainium2 kernel written in Bass

```python
import numpy as np
import jax
import jax.numpy as jnp

def _softmax(x, axis=-1):
    return jax.nn.softmax(x, axis=axis)

def _gelu(x):
    return jax.nn.gelu(x, approximate=True)

def _silu(x):
    return jax.nn.silu(x)

def _sigmoid(x):
    return jax.nn.sigmoid(x)

def _layernorm(x, axis=-1, eps=1e-05):
    m = jnp.mean(x, axis=axis, keepdims=True)
    v = jnp.var(x, axis=axis, keepdims=True)
    return (x - m) / jnp.sqrt(v + eps)

def _scatter_add(tgt, idx, src, axis=0):
    return tgt.at[idx].add(src)

def _segment_sum(src, seg, n):
    return jax.ops.segment_sum(src, seg, n)
kernel_name = 'mk_gnn_resnorm_d4_gnn_r32_327ad4'

def setup_inputs(seed: int=0):
    np.random.seed(seed)
    _w = jnp.asarray

    def _rec_inputs():
        import jax
        import jax.numpy as jnp
        _gk = jax.random.key(seed)
        x = -0.0003713 + 1 * jax.random.normal(jax.random.fold_in(_gk, 1), (3125, 128), jnp.float32)
        _s = jax.random.randint(jax.random.fold_in(_gk, 2), (25000,), 0, 3125, jnp.int32)
        _d = jax.random.randint(jax.random.fold_in(_gk, 3), (25000,), 0, 3125, jnp.int32)
        _loop = jnp.arange(3125, dtype=jnp.int32)
        src = jnp.concatenate([_s, _d, _loop])
        dst = jnp.concatenate([_d, _s, _loop])
        _o = jnp.argsort(dst, stable=True)
        src = src[_o]
        dst = dst[_o]
        edge_attr_128 = -4.21973e-05 + 0.999841 * jax.random.normal(jax.random.fold_in(_gk, 12), (53125, 128), jnp.float32)
        return (x, src, dst, edge_attr_128)
    x, src, dst, edge_attr_128 = _rec_inputs()

    def _L0_gnn_setup():
        import jax, jax.numpy as jnp
        import numpy as np
        N_NODES = 3125
        N_EDGES = 18750
        D_FEAT = 128
        key = jax.random.key(seed)
        k1, k2, k3 = jax.random.split(key, 3)
        r = jax.random.normal(k1, (N_NODES, D_FEAT), dtype=jnp.float32)
        e = jax.random.normal(k2, (N_EDGES, D_FEAT), dtype=jnp.float32)
        a = jax.random.randint(k3, (N_EDGES, 2), 0, N_NODES, dtype=jnp.int64)
        return {'r': r, 'e': e, 'a': a}
    _L0_gnn_all = _L0_gnn_setup()
    _L0_gnn_in = {k: v for k, v in _L0_gnn_all.items() if k in ()}
    del _L0_gnn_all

    def _L1_gnn_setup():
        import jax, jax.numpy as jnp
        import numpy as np
        N_NODES = 50000
        N_EDGES = 25000
        IN_FEATS = 128
        HEADS = 4
        OUT_FEATS = 32
        NEG_SLOPE = 0.2
        key = jax.random.key(seed)
        ks = jax.random.split(key, 8)
        feats = jax.random.normal(ks[0], (N_NODES, IN_FEATS), dtype=jnp.float32)
        src = jax.random.randint(ks[1], (N_EDGES,), 0, N_NODES, dtype=jnp.int32)
        dst = jax.random.randint(ks[2], (N_EDGES,), 0, N_NODES, dtype=jnp.int32)
        fc_w = jax.random.normal(ks[3], (IN_FEATS, HEADS * OUT_FEATS), dtype=jnp.float32) / np.sqrt(IN_FEATS)
        attn_l = jax.random.normal(ks[4], (HEADS, OUT_FEATS), dtype=jnp.float32) / np.sqrt(OUT_FEATS)
        attn_r = jax.random.normal(ks[5], (HEADS, OUT_FEATS), dtype=jnp.float32) / np.sqrt(OUT_FEATS)
        bias = jnp.zeros((HEADS * OUT_FEATS,), dtype=jnp.float32)
        return {'feats': feats, 'src': src, 'dst': dst, 'fc_w': fc_w, 'attn_l': attn_l, 'attn_r': attn_r, 'bias': bias}
    _L1_gnn_all = _L1_gnn_setup()
    _L1_gnn_in = {k: v for k, v in _L1_gnn_all.items() if k in ('fc_w', 'attn_l', 'attn_r', 'bias')}
    del _L1_gnn_all

    def _L2_gnn_setup():
        import jax, jax.numpy as jnp
        import numpy as np
        N_NODES = 50000
        N_EDGES = 25000
        IN_FEATS = 128
        OUT_FEATS = 128
        key = jax.random.key(seed)
        k1, k2, k3, k4 = jax.random.split(key, 4)
        feature = jax.random.normal(k1, (N_NODES, IN_FEATS), dtype=jnp.float32)
        src = jax.random.randint(k2, (N_EDGES,), 0, N_NODES, dtype=jnp.int64)
        dst = jax.random.randint(k3, (N_EDGES,), 0, N_NODES, dtype=jnp.int64)
        bound = 1.0 / np.sqrt(IN_FEATS)
        W = jax.random.uniform(k4, (OUT_FEATS, IN_FEATS), minval=-bound, maxval=bound, dtype=jnp.float32)
        b = jnp.zeros((OUT_FEATS,), dtype=jnp.float32)
        return {'feature': feature, 'src': src, 'dst': dst, 'W': W, 'b': b}
    _L2_gnn_all = _L2_gnn_setup()
    _L2_gnn_in = {k: v for k, v in _L2_gnn_all.items() if k in ('W', 'b')}
    del _L2_gnn_all

    def _L3_gnn_setup():
        import jax, jax.numpy as jnp
        import numpy as np
        N_NODES = 3125
        N_EDGES = 20000
        DIM = 128
        key = jax.random.key(seed)
        k1, k2, k3 = jax.random.split(key, 3)
        x = jax.random.normal(k1, (N_NODES, DIM), dtype=jnp.float32)
        edge_index = jax.random.randint(k2, (2, N_EDGES), 0, N_NODES, dtype=jnp.int64)
        W = jax.random.normal(k3, (DIM, DIM), dtype=jnp.float32) / np.sqrt(DIM)
        b = jnp.zeros((DIM,), dtype=jnp.float32)
        return {'x': x, 'edge_index': edge_index, 'W': W, 'b': b}
    _L3_gnn_all = _L3_gnn_setup()
    _L3_gnn_in = {k: v for k, v in _L3_gnn_all.items() if k in ('W', 'b')}
    del _L3_gnn_all
    return {'x': x, 'src': src, 'dst': dst, 'edge_attr_128': edge_attr_128, 'L1_gnn_fc_w': _L1_gnn_in['fc_w'], 'L1_gnn_attn_l': _L1_gnn_in['attn_l'], 'L1_gnn_attn_r': _L1_gnn_in['attn_r'], 'L1_gnn_bias': _L1_gnn_in['bias'], 'L2_gnn_W': _L2_gnn_in['W'], 'L2_gnn_b': _L2_gnn_in['b'], 'L3_gnn_W': _L3_gnn_in['W'], 'L3_gnn_b': _L3_gnn_in['b']}

def reference(x, src, dst, edge_attr_128, L1_gnn_fc_w, L1_gnn_attn_l, L1_gnn_attn_r, L1_gnn_bias, L2_gnn_W, L2_gnn_b, L3_gnn_W, L3_gnn_b):
    import jax
    import jax.numpy as jnp

    def _L0_gnn_ref(r, e, a):
        import jax, jax.numpy as jnp
        import numpy as np
        N_NODES = 3125
        N_EDGES = 18750
        D_FEAT = 128
        r1 = r[a[:, 0]] * e
        r2 = r[a[:, 1]] * e
        n = r.shape[0]
        out = jax.ops.segment_sum(r1, a[:, 1], num_segments=n)
        out = out + jax.ops.segment_sum(r2, a[:, 0], num_segments=n)
        return out

    def _L1_gnn_ref(feats, src, dst, fc_w, attn_l, attn_r, bias):
        import jax, jax.numpy as jnp
        import numpy as np
        N_NODES = 50000
        N_EDGES = 25000
        IN_FEATS = 128
        HEADS = 4
        OUT_FEATS = 32
        NEG_SLOPE = 0.2
        n = feats.shape[0]
        h = (feats @ fc_w).reshape(n, HEADS, OUT_FEATS)
        el = jnp.einsum('nhf,hf->nh', h, attn_l)
        er = jnp.einsum('nhf,hf->nh', h, attn_r)
        e = el[src] + er[dst]
        e = jnp.where(e > 0, e, NEG_SLOPE * e)
        m = jax.ops.segment_max(e, dst, num_segments=n)
        m = jnp.where(jnp.isfinite(m), m, 0.0)
        ee = jnp.exp(e - m[dst])
        s = jax.ops.segment_sum(ee, dst, num_segments=n)
        alpha = ee / jnp.maximum(s[dst], 1e-20)
        msgs = alpha[:, :, None] * h[src]
        rst = jax.ops.segment_sum(msgs, dst, num_segments=n)
        rst = rst + feats.reshape(n, HEADS, OUT_FEATS)
        rst = rst + bias.reshape(1, HEADS, OUT_FEATS)
        return rst.reshape(n, HEADS * OUT_FEATS)

    def _L2_gnn_ref(feature, src, dst, W, b):
        import jax, jax.numpy as jnp
        import numpy as np
        N_NODES = 50000
        N_EDGES = 25000
        IN_FEATS = 128
        OUT_FEATS = 128
        n_nodes = feature.shape[0]
        msgs = feature[src]
        agg = jax.ops.segment_sum(msgs, dst, num_segments=n_nodes)
        return jnp.einsum('ni,oi->no', agg, W) + b

    def _L3_gnn_ref(x, edge_index, W, b):
        import jax, jax.numpy as jnp
        import numpy as np
        N_NODES = 3125
        N_EDGES = 20000
        DIM = 128
        N = x.shape[0]
        loop = jnp.arange(N, dtype=edge_index.dtype)
        row = jnp.concatenate([edge_index[0], loop])
        col = jnp.concatenate([edge_index[1], loop])
        deg = jax.ops.segment_sum(jnp.ones_like(col, dtype=x.dtype), col, num_segments=N)
        dinv = jnp.where(deg > 0, jax.lax.rsqrt(deg), 0.0)
        norm = dinv[row] * dinv[col]
        h = x @ W
        msg = h[row] * norm[:, None]
        out = jax.ops.segment_sum(msg, col, num_segments=N)
        out = jax.nn.relu(out + b)
        return out
    edge_index = jnp.stack([src, dst])
    edge_index_t = jnp.stack([src, dst], axis=1)
    x = _layernorm(x + _L0_gnn_ref(x, edge_attr_128, edge_index_t), axis=-1)
    x = _layernorm(x + _L1_gnn_ref(x, src, dst, L1_gnn_fc_w, L1_gnn_attn_l, L1_gnn_attn_r, L1_gnn_bias), axis=-1)
    x = _layernorm(x + _L2_gnn_ref(x, src, dst, L2_gnn_W, L2_gnn_b), axis=-1)
    x = _layernorm(x + _L3_gnn_ref(x, edge_index, L3_gnn_W, L3_gnn_b), axis=-1)
    return x

_drawn_inputs = setup_inputs


def setup_inputs(seed=0):
    import zlib

    import numpy as np

    out = dict(_drawn_inputs(seed))
    spreads = {'L1_gnn_bias': (0.0, 0.1), 'L2_gnn_b': (0.0, 0.1), 'L3_gnn_b': (0.0, 0.1)}
    factors = {}
    for name, (base, spread) in spreads.items():
        noise = np.random.default_rng([zlib.crc32(name.encode()), seed]).standard_normal(out[name].shape)
        drawn = base * np.exp(spread * noise) if base else spread * noise
        out[name] = jnp.asarray(drawn.astype(out[name].dtype))
    for name, factor in factors.items():
        out[name] = (out[name] * factor).astype(out[name].dtype)
    return out
```

```python
from contextlib import ExitStack

import concourse.bass as bass
from concourse import mybir

ALU = mybir.AluOpType
ACT = mybir.ActivationFunctionType
AX_X = mybir.AxisListType.X
F32 = mybir.dt.float32
BF16 = mybir.dt.bfloat16
I32 = mybir.dt.int32
U32 = mybir.dt.uint32

P = 128
GROUP = 4
SIDES = 2
ROW = 132
SRC, DST_IN_BLOCK, SRC_SLOT, SRC_IN_BLOCK = 128, 129, 130, 131
EPS = 1e-5
FAR = 2.0 ** 100
SLOPE = 0.2
NOWHERE = 255


def gnn_program(nc, x, src, dst, edge_attr, fc_w, attn_l, attn_r, bias1, w2, b2, w3, b3, out):
    N, D = x.shape
    E = src.shape[0]
    HEADS, HF = attn_l.shape
    NB = -(-N // P)
    FULL = N // P
    REST = N - FULL * P
    NP_ = NB * P
    EP = 125
    ET = E // EP
    assert EP * ET == E and D == P and HEADS * HF == D
    NGROUP = 5
    NRING = 5
    NIT = ET // (NGROUP * NRING)
    assert NIT * NGROUP * NRING == ET
    STEP = GROUP * SIDES
    TILES = -(-((E + NB * P) // P) // STEP) * STEP
    IT = TILES // STEP
    SLOTS = TILES * P
    LW = D + HEADS + 1

    record = nc.dram_tensor("record", [SLOTS, ROW], F32, kind="Internal").ap()
    record2 = nc.dram_tensor("record2", [SLOTS, ROW], F32, kind="Internal").ap()
    stash = nc.dram_tensor("stash", [TILES, P, ROW], F32, kind="Internal").ap()
    table1 = nc.dram_tensor("table1", [NP_, ROW], F32, kind="Internal").ap()
    table2 = nc.dram_tensor("table2", [NP_, D], F32, kind="Internal").ap()
    table3 = nc.dram_tensor("table3", [NP_, D], F32, kind="Internal").ap()

    slots = record[0:SLOTS].rearrange("(k p) c -> p k c", p=P)
    slots2 = record2[0:SLOTS].rearrange("(k p) c -> p k c", p=P)
    stash_v = stash.rearrange("k p c -> p k c")
    edges = edge_attr.rearrange("(p t) f -> p t f", p=EP)

    with ExitStack() as ctx:
        def sb(name, shape, dt=F32):
            return ctx.enter_context(nc.sbuf_tensor(name, shape, dt))

        def sem(name):
            return ctx.enter_context(nc.semaphore(name))

        PS = ctx.enter_context(nc.psum_tensor("PS", [P, 8, 512], F32))

        lane_i = sb("lane_i", [P, 1], I32)
        lane = sb("lane", [P, 1])
        iota_i = sb("iota_i", [P, P], I32)
        iota = sb("iota", [P, P])
        ident = sb("ident", [P, P])
        before = sb("before", [P, P])
        ones = sb("ones", [P, P])
        far_id = sb("far_id", [P, P], BF16)
        tile_no_i = sb("tile_no_i", [P, GROUP], I32)
        tile_no = sb("tile_no", [P, GROUP])
        pad_i = sb("pad_i", [P, 1], I32)
        pad = sb("pad", [P, STEP, ROW])
        fcw = sb("fcw", [P, D])
        w2n = sb("w2n", [P, D])
        w2t = sb("w2t", [P, D])
        w3n = sb("w3n", [P, D])
        al_row = sb("al_row", [P, D])
        ar_row = sb("ar_row", [P, D])
        b1_row = sb("b1_row", [P, D])
        b2_row = sb("b2_row", [P, D])
        b3_row = sb("b3_row", [P, D])

        ends = [sb("dst_e", [EP, ET], I32), sb("src_e", [EP, ET], I32)]
        blk_i = sb("blk_i", [EP, ET], I32)
        blk = sb("blk", [EP, ET])
        end_f = sb("end_f", [EP, ET])
        pos = sb("pos", [EP, ET])
        mask = sb("mask", [EP, NB, ET])
        shared = sb("shared", [P, NB * ET])
        run = shared[0:EP, :].rearrange("p (b t) -> p b t", t=ET)
        slot_d = sb("slot_d", [EP, ET], U32)
        meta = sb("meta", [EP, ET, 4], I32)
        upto = sb("upto", [EP, NB])
        cnt = sb("cnt", [EP, NB])
        base = sb("base", [EP, NB])
        tot_i = sb("tot_i", [P, NB], I32)
        ntile = sb("ntile", [P, NB])
        last = sb("last", [P, NB])
        first = sb("first", [P, NB])
        past = sb("past", [P, GROUP, NB])
        tblk = sb("tblk", [P, GROUP])
        tblk_i = [sb("tblk_d", [P, GROUP], I32), sb("tblk_s", [P, GROUP], I32)]
        block_of = [sb("block_of_d", [1, TILES], I32), sb("block_of_s", [1, TILES], I32)]

        NR = sb("NR", [EP, NRING, NGROUP, ROW])
        NX = sb("NX", [EP, NRING, NGROUP], U32)
        R = sb("R", [P, SIDES, GROUP, ROW])
        G = sb("G", [P, SIDES, GROUP, ROW])
        M = sb("M", [P, SIDES, GROUP, ROW])
        M1 = sb("M1", [P, SIDES, GROUP, D])
        OH = sb("OH", [P, SIDES, GROUP, P])
        OHT = sb("OHT", [P, SIDES, GROUP * P])
        NOT = sb("NOT", [P, SIDES, GROUP, P], BF16)
        IX = sb("IX", [P, SIDES, GROUP], U32)
        S = sb("S", [P, SIDES, GROUP, LW])
        logit = sb("logit", [P, SIDES, GROUP, HEADS])
        slope = sb("slope", [P, SIDES, GROUP, HEADS])
        shift = sb("shift", [P, SIDES, GROUP, HEADS])
        tmax = sb("tmax", [P, SIDES, GROUP, HEADS])
        src_of = sb("src_of", [P, TILES], U32)
        dloc = sb("dloc", [P, TILES])

        X = sb("X", [P, NB * D])
        X3 = X[:, :].rearrange("p (b f) -> p b f", f=D)
        o1, o2, o3 = NB * D, NB * (D + LW), NB * (D + LW + ROW)
        Y = shared[:, 0:o1].rearrange("p (b f) -> p b f", f=D)
        acc = sb("acc", [P, NB, D])
        acc_flat = acc[:, :, :].rearrange("p b f -> p (b f)")
        acc1 = shared[:, o1:o2].rearrange("p (b f) -> p b f", f=LW)
        acc1_flat = shared[:, o1:o2]
        HL = shared[:, o2:o3].rearrange("p (b f) -> p b f", f=ROW)
        erm = sb("erm", [P, NB, 2 * HEADS])
        erm_flat = erm[:, :, :].rearrange("p b f -> p (b f)")
        elmax = sb("elmax", [P, NB, HEADS])
        elmax_flat = elmax[:, :, :].rearrange("p b f -> p (b f)")
        stage = sb("stage", [P, 5, D])
        xt = sb("xt", [P, 5 * P])
        nsum = sb("nsum", [P, NB])
        nvar = sb("nvar", [P, NB])
        rstd = sb("rstd", [P, NB])
        dinv = sb("dinv", [P, NB])
        small = sb("small", [P, NB, HEADS])

        s_w = sem("weights_loaded")
        s_x = sem("x_loaded")
        s_ends = sem("ends_loaded")
        s_iota = sem("iotas_made")
        s_dv = sem("vector_chain")
        s_gate = sem("pool_gate")
        s_pad = sem("pad_made")
        s_blank = sem("record_blank")
        s_blank2 = sem("record2_blank")
        s_cnt = sem("counts_made")
        s_tot = sem("counts_summed")
        s_tb = sem("tile_blocks_made")
        s_tbl = sem("tile_blocks_laid")
        s_clear = sem("x_padding_cleared")
        s_w2 = sem("w2_turned")
        s_nload = [sem(f"edges_loaded{g}") for g in range(NRING)]
        s_nmeta = sem("meta_filled")
        s_nput = [sem(f"edges_put{g}") for g in range(NRING)]

        class Sems:
            def __init__(self, name):
                self.load = [sem(f"{name}_loaded{g}") for g in range(SIDES)]
                self.gather = [sem(f"{name}_gathered{g}") for g in range(SIDES)]
                self.put = [sem(f"{name}_put{g}") for g in range(SIDES)]
                self.ix = sem(f"{name}_indices")
                self.onehot = sem(f"{name}_onehot")
                self.turned = sem(f"{name}_turned")
                self.onehot_t = sem(f"{name}_onehot_t")
                self.looked = sem(f"{name}_looked_up")
                self.scaled = sem(f"{name}_scaled")
                self.summed = sem(f"{name}_summed")
                self.added = sem(f"{name}_added")

        a = Sems("a")
        c = Sems("c")
        m = Sems("m")
        w = Sems("w")
        l2, l3 = Sems("l2"), Sems("l3")
        s_m2 = sem("a_source_messages")
        s_mx = sem("m_tile_max")
        s_lg = sem("w_logit")
        s_lk = sem("w_leaky")
        s_lg2 = sem("w_less_maximum")
        s_sh = sem("w_shifted")
        s_ex = sem("w_exp")

        s_nx = sem("nodes_ready")
        s_nt = sem("nodes_turned")
        s_ntc = sem("nodes_turned_copied")
        s_nm = sem("nodes_multiplied")
        s_nd = sem("nodes_taken")
        s_var = sem("variance_ready")
        s_std = sem("deviation_ready")
        s_tab = [sem(f"table{n}_ready") for n in range(3)]
        s_tabw = [sem(f"table{n}_written") for n in range(3)]
        s_fin = sem("result_ready")
        s_out = sem("result_written")

        block = ctx.enter_context(nc.Block())

        def again(i):
            return not (isinstance(i, int) and i == 0)

        def turns(eng, n, body):
            body(0)
            with eng.Fori(1, n) as i:
                body(i)

        def ahead(eng, n, early, late):
            early(0, 0)
            early(0, 1)
            late(0, 0)
            early(1, 0)
            late(0, 1)
            with eng.Fori(1, n - 1) as i:
                early(i, 1)
                late(i, 0)
                early(i + 1, 0)
                late(i, 1)
            early(n - 1, 1)
            late(n - 1, 0)
            late(n - 1, 1)

        def blocks_of(eng_type, table, t0):
            _, regs = nc.values_load_multi_w_load_instructions(
                table[0:1, bass.ds(t0, GROUP)], engines=[eng_type], min_val=0, max_val=NB - 1,
                skip_runtime_bounds_check_because="the table is clamped to the last block")
            return regs

        @block.sync
        def _(sp):
            for e, given in zip(ends, (dst, src)):
                sp.dma_start(e[:, :], given.rearrange("(p t) -> p t", p=EP)).then_inc(s_ends, 16)
            sp.dma_start(X3[:, 0:FULL, :], x[0:FULL * P, :].rearrange("(b p) f -> p b f", p=P)).then_inc(s_x, 16)
            sp.wait_ge(s_clear, 1)
            sp.dma_start(X3[0:REST, FULL, :], x[FULL * P:N, :]).then_inc(s_x, 16)
            for t, given in ((fcw, fc_w), (w2n, w2), (w3n, w3)):
                sp.dma_start(t[:, :], given).then_inc(s_w, 16)
            for t, given in ((al_row, attn_l.rearrange("h f -> (h f)")), (ar_row, attn_r.rearrange("h f -> (h f)")),
                             (b1_row, bias1), (b2_row, b2), (b3_row, b3)):
                sp.dma_start(t[:, :], given.partition_broadcast(P)).then_inc(s_w, 16)
            sp.wait_ge(s_pad, 1)
            for rec, s in ((slots, s_blank), (slots2, s_blank2)):
                with sp.Fori(0, IT) as i:
                    sp.dma_start(rec[:, bass.ds(STEP * i, STEP), :], pad[:, :, :]).then_inc(s, 16)
            for n in range(2):
                sp.wait_ge(s_tb, n + 1)
                sp.dma_start(block_of[n][0:1, :].rearrange("a (p q) -> a p q", q=GROUP),
                             tblk_i[n][0:TILES // GROUP, :]).then_inc(s_tbl, 16)

            def load_edges(i):
                for g in range(NRING):
                    if again(i):
                        sp.wait_ge(s_nput[g], 16 * NGROUP * i)
                    sp.dma_start(NR[:, g, :, 0:D],
                                 edges[:, bass.ds((i * NRING + g) * NGROUP, NGROUP), :]).then_inc(s_nload[g], 16)
            turns(sp, NIT, load_edges)
            for g in range(NRING):
                sp.wait_ge(s_nput[g], 16 * NGROUP * NIT)

            def load_records(i):
                for g in range(SIDES):
                    if again(i):
                        sp.wait_ge(s_m2, SIDES * (i - 1) + g + 1)
                    sp.dma_start(R[:, g, :, :], slots[:, bass.ds(STEP * i + GROUP * g, GROUP), :]).then_inc(a.load[g], 16)
            turns(sp, IT, load_records)

            for g in range(SIDES):
                sp.wait_ge(a.put[g], 16 * GROUP * IT)

            def load_records2(i):
                for g in range(SIDES):
                    if again(i):
                        sp.wait_ge(c.summed, SIDES * (i - 1) + g + 1)
                    sp.dma_start(R[:, g, :, :], slots2[:, bass.ds(STEP * i + GROUP * g, GROUP), :]).then_inc(c.load[g], 16)
            turns(sp, IT, load_records2)

            sp.wait_ge(s_tab[0], 1)
            sp.dma_start(table1.rearrange("(b p) c -> p b c", p=P), HL[:, :, :]).then_inc(s_tabw[0], 16)

            def keep_rows(i):
                for g in range(SIDES):
                    sp.wait_ge(m.gather[g], 16 * GROUP * (i + 1))
                    sp.dma_start(stash_v[:, bass.ds(STEP * i + GROUP * g, GROUP), :], G[:, g, :, :]).then_inc(m.put[g], 16)
            turns(sp, IT, keep_rows)
            for g in range(SIDES):
                sp.wait_ge(m.put[g], 16 * IT)

            def load_rows(i):
                for g in range(SIDES):
                    if again(i):
                        sp.wait_ge(w.summed, SIDES * (i - 1) + g + 1)
                    sp.dma_start(S[:, g, :, 0:ROW],
                                 stash_v[:, bass.ds(STEP * i + GROUP * g, GROUP), :]).then_inc(w.load[g], 16)
            sp.wait_ge(s_tab[0], 2)
            turns(sp, IT, load_rows)

            sp.wait_ge(s_tab[1], 1)
            sp.dma_start(table2.rearrange("(b p) c -> p b c", p=P), X3).then_inc(s_tabw[1], 16)
            sp.wait_ge(s_tab[2], 1)
            sp.dma_start(table3.rearrange("(b p) c -> p b c", p=P), Y[:, :, :]).then_inc(s_tabw[2], 16)
            sp.wait_ge(s_fin, 1)
            sp.dma_start(out[0:FULL * P, :].rearrange("(b p) f -> p b f", p=P), X3[:, 0:FULL, :]).then_inc(s_out, 16)
            sp.dma_start(out[FULL * P:N, :], X3[0:REST, FULL, :]).then_inc(s_out, 16)
            sp.wait_ge(s_out, 32)
            sp.wait_ge(s_blank, 16 * IT)
            sp.wait_ge(s_blank2, 16 * IT)
            for n in range(3):
                sp.wait_ge(s_tabw[n], 16)

        @block.gpsimd
        def _(pool):
            def row_index(ap):
                return bass.IndirectOffsetOnAxis(ap, 0)

            pool.iota(iota_i[:, :], [[1, P]], base=0, channel_multiplier=0).then_inc(s_iota, 1)
            pool.iota(lane_i[:, :], [[0, 1]], base=0, channel_multiplier=1).then_inc(s_iota, 1)
            pool.iota(tile_no_i[:, :], [[1, GROUP]], base=0, channel_multiplier=GROUP).then_inc(s_iota, 1)
            pool.iota(pad_i[:, :], [[0, 1]], base=SLOTS, channel_multiplier=0).then_inc(s_iota, 1)
            pool.memset(pad[:, :, :], 0.0).then_inc(s_iota, 1)

            pool.wait_ge(s_blank, 16 * IT)

            def put_edges(i):
                for g in range(NRING):
                    pool.wait_ge(s_nload[g], 16 * (i + 1))
                    pool.wait_ge(s_nmeta, NRING * i + g + 1)
                    pool.sem_inc(s_gate, 1)
                    for j in range(NGROUP):
                        pool.indirect_dma_start(record[:, :], row_index(NX[:, g, j:j + 1]), NR[:, g, j, :],
                                                None).then_inc(s_nput[g], 16)
            turns(pool, NIT, put_edges)
            pool.wait_ge(s_blank2, 16 * IT)

            def gather_x(i, g):
                pool.wait_ge(a.load[g], 16 * (i + 1))
                if again(i):
                    pool.wait_ge(a.scaled, SIDES * (i - 1) + g + 1)
                pool.sem_inc(s_gate, 1)
                for j in range(GROUP):
                    pool.indirect_dma_start(G[:, g, j, 0:D], None, x[:, :],
                                            row_index(R[:, g, j, SRC:SRC + 1].bitcast(U32))).then_inc(a.gather[g], 16)

            def put_messages(i, g):
                pool.wait_ge(s_m2, SIDES * i + g + 1)
                pool.sem_inc(s_gate, 1)
                for j in range(GROUP):
                    pool.indirect_dma_start(record2[:, :], row_index(IX[:, g, j:j + 1]),
                                            M[:, g, j, :], None, bounds_check=SLOTS - 1,
                                            oob_is_err=False).then_inc(a.put[g], 16)
            ahead(pool, IT, gather_x, put_messages)

            def gather_rows(p, table, width, free, per):
                def step(i):
                    for g in range(SIDES):
                        if again(i):
                            pool.wait_ge(p.gather[g], 16 * GROUP * i)
                            pool.sem_inc(s_gate, 1)
                        pool.tensor_copy(IX[:, g, :], src_of[:, bass.ds(STEP * i + GROUP * g, GROUP)]).then_inc(p.ix, 1)
                        pool.wait_ge(p.ix, SIDES * i + g + 1)
                        if again(i):
                            pool.wait_ge(free, per * (SIDES * (i - 1) + g + 1))
                            if p is m:
                                pool.wait_ge(m.put[g], 16 * i)
                        pool.sem_inc(s_gate, 1)
                        for j in range(GROUP):
                            pool.indirect_dma_start(G[:, g, j, 0:width], None, table[:, :],
                                                    row_index(IX[:, g, j:j + 1])).then_inc(p.gather[g], 16)
                turns(pool, IT, step)

            for g in range(SIDES):
                pool.wait_ge(a.put[g], 16 * GROUP * IT)
            pool.wait_ge(s_tabw[0], 16)
            gather_rows(m, table1, ROW, m.summed, GROUP)
            for g in range(SIDES):
                pool.wait_ge(m.put[g], 16 * IT)
            pool.wait_ge(s_tabw[1], 16)
            gather_rows(l2, table2, D, l2.summed, 1)
            pool.wait_ge(s_tabw[2], 16)
            gather_rows(l3, table3, D, l3.summed, 1)

        @block.tensor
        def _(pe):
            for n in range(2):
                pe.wait_ge(s_cnt, n + 1)
                pe.matmul(PS[0:EP, 0, 0:NB], before[0:EP, 0:EP], cnt[:, :], start=True, stop=True)
                pe.matmul(PS[:, 1, 0:NB], ones[0:EP, :], cnt[:, :], start=True, stop=True).then_inc(s_tot, 1)
            pe.wait_ge(s_w, 16 * 8)
            pe.transpose(PS[:, 7, 0:P], w2n[:, :], ident[:, :]).then_inc(s_w2, 1)

            def turn_onehot(p, i, g):
                pe.wait_ge(p.onehot, SIDES * i + g + 1)
                if again(i):
                    pe.wait_ge(p.onehot_t, SIDES * (i - 1) + g + 1)
                for j in range(GROUP):
                    t = pe.transpose(PS[:, g, j * P:(j + 1) * P], OH[:, g, j, :], ident[:, :])
                t.then_inc(p.turned, 1)

            def sum_rows(p, rows, i, g):
                if again(i):
                    pe.wait_ge(p.added, GROUP * (SIDES * (i - 1) + g + 1))
                for j in range(GROUP):
                    t = pe.matmul(PS[:, 4 + g, j * P:(j + 1) * P], OH[:, g, j, :], rows[:, g, j, 0:D],
                                  start=True, stop=True)
                t.then_inc(p.summed, 1)

            pe.wait_ge(s_tbl, 32)
            pe.wait_ge(s_x, 32)

            def early(i, g):
                turn_onehot(a, i, g)
                regs = blocks_of(mybir.EngineType.PE, block_of[0], STEP * i + GROUP * g)
                pe.wait_ge(a.onehot_t, SIDES * i + g + 1)
                if again(i):
                    pe.wait_ge(s_m2, SIDES * (i - 1) + g + 1)
                for j in range(GROUP):
                    t = pe.matmul(PS[:, 2 + g, j * P:(j + 1) * P], OHT[:, g, j * P:(j + 1) * P],
                                  X[:, bass.ds(regs[j] * D, D)], start=True, stop=True)
                t.then_inc(a.looked, 1)

            def late(i, g):
                pe.wait_ge(a.scaled, SIDES * i + g + 1)
                sum_rows(a, M1, i, g)

            def layer0(i):
                for g in range(SIDES):
                    early(i, g)
                    late(i, g)
            turns(pe, IT, layer0)

            def plain(p, rows, arrived, per):
                def step(i):
                    for g in range(SIDES):
                        pe.wait_ge(p.onehot, SIDES * i + g + 1)
                        pe.wait_ge(arrived[g], per * (i + 1))
                        sum_rows(p, rows, i, g)
                turns(pe, IT, step)
            plain(c, R, c.load, 16)

            def five(weights, turn):
                with pe.Fori(0, NB // 5) as i:
                    n = i + turn * (NB // 5)
                    pe.wait_ge(s_nx, n + 1)
                    for b in range(5):
                        t = pe.transpose(PS[:, b // 4, (b % 4) * P:(b % 4 + 1) * P], stage[:, b, :], ident[:, :])
                    t.then_inc(s_nt, 1)
                    pe.wait_ge(s_ntc, n + 1)
                    for b in range(5):
                        t = pe.matmul(PS[:, 2 + b // 4, (b % 4) * P:(b % 4 + 1) * P], xt[:, b * P:(b + 1) * P],
                                      weights[:, :], start=True, stop=True)
                    t.then_inc(s_nm, 1)
            five(fcw, 0)

            def maxima(i):
                for g in range(SIDES):
                    pe.wait_ge(m.onehot, SIDES * i + g + 1)
                    pe.wait_ge(m.gather[g], 16 * GROUP * (i + 1))
                    for j in range(GROUP):
                        if again(i):
                            pe.wait_ge(s_mx, STEP * (i - 1) + GROUP * g + j + 1)
                        bank = PS[:, g * GROUP + j, :]
                        for h in range(HEADS):
                            pe.matmul(bank[:, h * P:(h + 1) * P], NOT[:, g, j, :], far_id[:, :], start=True, stop=False)
                            t = pe.matmul(bank[:, h * P:(h + 1) * P], G[:, g, j, D + h:D + h + 1].to_broadcast([P, P]),
                                          ident[:, :], start=False, stop=True)
                        t.then_inc(m.summed, 1)
            turns(pe, IT, maxima)

            pe.wait_ge(s_tab[0], 3)

            def messages(i):
                for g in range(SIDES):
                    turn_onehot(w, i, g)
                    regs = blocks_of(mybir.EngineType.PE, block_of[0], STEP * i + GROUP * g)
                    pe.wait_ge(w.onehot_t, SIDES * i + g + 1)
                    if again(i):
                        pe.wait_ge(s_sh, SIDES * (i - 1) + g + 1)
                    for j in range(GROUP):
                        t = pe.matmul(PS[:, 2 + g, 8 * j:8 * j + 8], OHT[:, g, j * P:(j + 1) * P],
                                      erm_flat[:, bass.ds(regs[j] * (2 * HEADS), 2 * HEADS)], start=True, stop=True)
                    t.then_inc(w.looked, 1)
                    pe.wait_ge(w.scaled, SIDES * i + g + 1)
                    if again(i):
                        pe.wait_ge(w.added, GROUP * (SIDES * (i - 1) + g + 1))
                    for j in range(GROUP):
                        t = pe.matmul(PS[:, 4 + 2 * g + j // 2, (j % 2) * 256:(j % 2) * 256 + LW], OH[:, g, j, :],
                                      S[:, g, j, :], start=True, stop=True)
                    t.then_inc(w.summed, 1)
            turns(pe, IT, messages)

            plain(l2, G, l2.gather, 16 * GROUP)
            five(w2t, 1)
            plain(l3, G, l3.gather, 16 * GROUP)
            five(w3n, 2)

        @block.scalar
        def _(act):
            def copy_turned(p):
                def step(i):
                    for g in range(SIDES):
                        act.wait_ge(p.turned, SIDES * i + g + 1)
                        if again(i):
                            act.wait_ge(p.looked, SIDES * (i - 1) + g + 1)
                        act.activation(OHT[:, g, :], PS[:, g, :], ACT.Copy).then_inc(p.onehot_t, 1)
                return step

            def five(turn):
                with act.Fori(0, NB // 5) as i:
                    n = i + turn * (NB // 5)
                    act.wait_ge(s_nt, n + 1)
                    act.activation(xt[:, 0:4 * P], PS[:, 0, :], ACT.Copy)
                    act.activation(xt[:, 4 * P:5 * P], PS[:, 1, 0:P], ACT.Copy).then_inc(s_ntc, 1)

            def root(n):
                act.wait_ge(s_var, n)
                act.activation(nvar[:, :], nvar[:, :], ACT.Sqrt).then_inc(s_std, 1)

            turns(act, IT, copy_turned(a))
            root(1)
            five(0)
            def weights_step(i):
                for g in range(SIDES):
                    act.wait_ge(w.turned, SIDES * i + g + 1)
                    if again(i):
                        act.wait_ge(w.looked, SIDES * (i - 1) + g + 1)
                    act.activation(OHT[:, g, :], PS[:, g, :], ACT.Copy).then_inc(w.onehot_t, 1)
                    act.wait_ge(s_sh, SIDES * i + g + 1)
                    act.activation(S[:, g, :, D:D + HEADS], shift[:, g, :, :], ACT.Exp).then_inc(s_ex, 1)
            turns(act, IT, weights_step)
            act.wait_ge(s_var, 2)
            act.activation(dinv[:, :], dinv[:, :], ACT.Sqrt).then_inc(s_std, 1)
            root(3)
            five(1)
            root(4)
            five(2)
            root(5)

        @block.vector
        def _(dve):
            done = [0]

            def link(ins):
                done[0] += 1
                ins.then_inc(s_dv, 1)
                dve.wait_ge(s_dv, done[0])

            dve.memset(X3[:, FULL, :], 0.0).then_inc(s_clear, 1)
            dve.wait_ge(s_iota, 5)
            link(dve.tensor_copy(iota[:, :], iota_i[:, :]))
            link(dve.tensor_copy(lane[:, :], lane_i[:, :]))
            link(dve.tensor_copy(tile_no[:, :], tile_no_i[:, :]))
            link(dve.tensor_scalar(ident[:, :], iota[:, :], lane[:, 0:1], None, ALU.is_equal))
            dve.tensor_scalar(before[:, :], iota[:, :], lane[:, 0:1], None, ALU.is_gt)
            dve.memset(ones[:, :], 1.0)
            dve.tensor_scalar(far_id[:, :], ident[:, :], FAR, None, ALU.mult)
            pad_int = pad[:, :, :].bitcast(I32)
            for col in (DST_IN_BLOCK, SRC_IN_BLOCK):
                link(dve.tensor_scalar(pad_int[:, :, col], pad_int[:, :, 0], float(NOWHERE), None, ALU.add))
            dve.tensor_copy(pad_int[:, :, SRC_SLOT], pad_i[:, 0:1].to_broadcast([P, STEP])).then_inc(s_pad, 1)

            dve.wait_ge(s_ends, 32)
            for n in range(2):
                link(dve.tensor_copy(end_f[:, :], ends[n][:, :]))
                link(dve.tensor_scalar(blk_i[:, :], ends[n][:, :], 7, None, ALU.arith_shift_right))
                link(dve.tensor_copy(blk[:, :], blk_i[:, :]))
                col = (DST_IN_BLOCK, SRC_IN_BLOCK)[n] - D
                link(dve.scalar_tensor_tensor(meta[:, :, col], blk[:, :], -float(P), end_f[:, :], ALU.mult, ALU.add))
                if n == 1:
                    link(dve.tensor_copy(meta[:, :, SRC - D], ends[1][:, :]))
                link(dve.tensor_tensor(mask[:, :, :], blk[:, :].unsqueeze(1).to_broadcast([EP, NB, ET]),
                                       iota[0:EP, 0:NB].unsqueeze(2).to_broadcast([EP, NB, ET]), ALU.is_equal))
                flat_run = shared[0:EP, :]
                flat_mask = mask[:, :, :].rearrange("p b t -> p (b t)")
                link(dve.tensor_tensor_scan(flat_run, flat_mask, flat_mask, 0.0, ALU.add, ALU.max))
                link(dve.tensor_copy(upto[:, :], run[:, :, ET - 1]))
                link(dve.tensor_copy(cnt[:, 0:1], upto[:, 0:1]))
                dve.tensor_tensor(cnt[:, 1:NB], upto[:, 1:NB], upto[:, 0:NB - 1], ALU.subtract).then_inc(s_cnt, 1)
                dve.wait_ge(s_tot, n + 1)
                link(dve.tensor_scalar(tot_i[:, :], PS[:, 1, 0:NB], float(P - 1), None, ALU.add))
                link(dve.tensor_scalar(tot_i[:, :], tot_i[:, :], 7, None, ALU.arith_shift_right))
                link(dve.tensor_scalar(ntile[:, :], tot_i[:, :], 1.0, None, ALU.max))
                link(dve.tensor_tensor_scan(last[:, :], ntile[:, :], ntile[:, :], 0.0, ALU.add, ALU.max))
                link(dve.tensor_tensor(first[:, :], last[:, :], ntile[:, :], ALU.subtract))
                link(dve.scalar_tensor_tensor(base[:, :], first[0:EP, :], float(P), PS[0:EP, 0, 0:NB],
                                              ALU.mult, ALU.add))
                link(dve.tensor_tensor(base[:, :], base[:, :], upto[:, :], ALU.subtract))
                link(dve.tensor_tensor(base[:, :], base[:, :], cnt[:, :], ALU.add))
                link(dve.tensor_scalar(base[:, :], base[:, :], -1.0, None, ALU.add))
                link(dve.tensor_tensor(run[:, :, :], run[:, :, :], base[:, :].unsqueeze(2).to_broadcast([EP, NB, ET]),
                                       ALU.add))
                link(dve.tensor_tensor(run[:, :, :], run[:, :, :], mask[:, :, :], ALU.mult))
                link(dve.tensor_reduce(pos[:, :], run[:, :, :].rearrange("p b t -> p t b"), AX_X, ALU.add))
                if n == 0:
                    link(dve.tensor_copy(slot_d[:, :], pos[:, :]))
                else:
                    link(dve.tensor_copy(meta[:, :, SRC_SLOT - D], pos[:, :]))
                link(dve.tensor_tensor(past[:, :, :], tile_no[:, :].unsqueeze(2).to_broadcast([P, GROUP, NB]),
                                       last[:, :].unsqueeze(1).to_broadcast([P, GROUP, NB]), ALU.is_ge))
                link(dve.tensor_reduce(tblk[:, :], past[:, :, :], AX_X, ALU.add))
                dve.tensor_scalar(tblk_i[n][:, :], tblk[:, :], float(NB - 1), None, ALU.min).then_inc(s_tb, 1)

            def fill_meta(i):
                for g in range(NRING):
                    if again(i):
                        dve.wait_ge(s_nput[g], 16 * NGROUP * i)
                    t0 = (i * NRING + g) * NGROUP
                    dve.tensor_copy(NR[:, g, :, D:ROW].bitcast(I32), meta[:, bass.ds(t0, NGROUP), :])
                    dve.tensor_copy(NX[:, g, :], slot_d[:, bass.ds(t0, NGROUP)]).then_inc(s_nmeta, 1)
            turns(dve, NIT, fill_meta)

            dve.wait_ge(s_w2, 1)
            link(dve.tensor_copy(w2t[:, :], PS[:, 7, 0:P]))
            link(dve.memset(acc[:, :, :], 0.0))
            link(dve.memset(acc1[:, :, :], 0.0))
            link(dve.memset(elmax[:, :, :], -3.0e38))
            dve.wait_ge(s_tbl, 32)
            dve.wait_ge(s_x, 32)

            def after_tile_before(p, i, g, j):
                if again(i) or g + j > 0:
                    dve.wait_ge(p.added, STEP * i + GROUP * g + j)

            def add_tiles(p, table, i, g):
                regs = blocks_of(mybir.EngineType.DVE, table, STEP * i + GROUP * g)
                dve.wait_ge(p.summed, SIDES * i + g + 1)
                for j in range(GROUP):
                    at = acc_flat[:, bass.ds(regs[j] * D, D)]
                    after_tile_before(p, i, g, j)
                    dve.tensor_tensor(at, PS[:, 4 + g, j * P:(j + 1) * P], at, ALU.add).then_inc(p.added, 1)

            def layer0(i):
                for g in range(SIDES):
                    t0 = STEP * i + GROUP * g
                    Ri = R[:, g, :, :].bitcast(I32)
                    dve.wait_ge(a.load[g], 16 * (i + 1))
                    if again(i):
                        dve.wait_ge(a.summed, SIDES * (i - 1) + g + 1)
                    for j in range(GROUP):
                        t = dve.tensor_scalar(OH[:, g, j, :], iota[:, :], R[:, g, j, DST_IN_BLOCK:DST_IN_BLOCK + 1].bitcast(I32),
                                              None, ALU.is_equal)
                    t.then_inc(a.onehot, 1)
                    dve.tensor_copy(src_of[:, bass.ds(t0, GROUP)], Ri[:, :, SRC])
                    dve.tensor_copy(dloc[:, bass.ds(t0, GROUP)], Ri[:, :, DST_IN_BLOCK])
                    dve.wait_ge(a.gather[g], 16 * GROUP * (i + 1))
                    dve.tensor_tensor(M1[:, g, :, :], G[:, g, :, 0:D], R[:, g, :, 0:D], ALU.mult).then_inc(a.scaled, 1)
                    if again(i):
                        dve.wait_ge(a.put[g], 16 * GROUP * i)
                    dve.tensor_copy(M[:, g, :, D:ROW].bitcast(I32), Ri[:, :, D:ROW])
                    dve.tensor_copy(IX[:, g, :], Ri[:, :, SRC_SLOT])
                    dve.wait_ge(a.looked, SIDES * i + g + 1)
                    dve.tensor_tensor(M[:, g, :, 0:D], PS[:, 2 + g, :].rearrange("p (j f) -> p j f", f=D),
                                      R[:, g, :, 0:D], ALU.mult).then_inc(s_m2, 1)
                    add_tiles(a, block_of[0], i, g)
            turns(dve, IT, layer0)

            def onehots(p, i, g):
                if again(i):
                    dve.wait_ge(p.summed, SIDES * (i - 1) + g + 1)
                for j in range(GROUP):
                    t = dve.tensor_scalar(OH[:, g, j, :], iota[:, :], dloc[:, bass.ds(STEP * i + GROUP * g + j, 1)],
                                          None, ALU.is_equal)
                t.then_inc(p.onehot, 1)

            def early(i, g):
                dve.wait_ge(c.load[g], 16 * (i + 1))
                if again(i):
                    dve.wait_ge(c.summed, SIDES * (i - 1) + g + 1)
                for j in range(GROUP):
                    t = dve.tensor_scalar(OH[:, g, j, :], iota[:, :], R[:, g, j, SRC_IN_BLOCK:SRC_IN_BLOCK + 1].bitcast(I32),
                                          None, ALU.is_equal)
                t.then_inc(c.onehot, 1)
            ahead(dve, IT, early, lambda i, g: add_tiles(c, block_of[1], i, g))
            dve.wait_ge(c.added, TILES)

            nroot = [0]

            def norm(to):
                link(dve.tensor_reduce(nsum[:, :], X3, AX_X, ALU.add))
                link(dve.tensor_scalar(nsum[:, :], nsum[:, :], 1.0 / D, None, ALU.mult))
                link(dve.tensor_tensor(X3, X3, nsum[:, :].unsqueeze(2).to_broadcast([P, NB, D]), ALU.subtract))
                link(dve.tensor_tensor(acc[:, :, :], X3, X3, ALU.mult))
                link(dve.tensor_reduce(nsum[:, :], acc[:, :, :], AX_X, ALU.add))
                nroot[0] += 1
                dve.tensor_scalar(nvar[:, :], nsum[:, :], 1.0 / D, EPS, ALU.mult, ALU.add).then_inc(s_var, 1)
                dve.wait_ge(s_std, nroot[0])
                link(dve.reciprocal(rstd[:, :], nvar[:, :]))
                link(dve.tensor_tensor(to, X3, rstd[:, :].unsqueeze(2).to_broadcast([P, NB, D]), ALU.mult))

            def heads(ap):
                return ap.rearrange("p (h f) -> p h f", h=HEADS)

            link(dve.tensor_tensor(X3, X3, acc[:, :, :], ALU.add))
            norm(X3)

            dve.wait_ge(s_w, 16 * 8)

            def five(turn, frm, take):
                with dve.Fori(0, NB // 5) as i:
                    n = i + turn * (NB // 5)
                    dve.tensor_copy(stage[:, :, :].rearrange("p b f -> p (b f)"),
                                    frm[:, bass.ds(i * (5 * D), 5 * D)]).then_inc(s_nx, 1)
                    dve.wait_ge(s_nm, n + 1)
                    take(i)

            psum5 = PS[:, 2:4, :].rearrange("p k c -> p (k c)")[:, 0:5 * D]
            Yf = shared[:, 0:o1]

            def take(i):
                dve.tensor_copy(Yf[:, bass.ds(i * (5 * D), 5 * D)], psum5).then_inc(s_nd, 1)
            five(0, X, take)
            dve.wait_ge(s_nd, NB // 5)
            link(dve.tensor_copy(HL[:, :, 0:D], Y[:, :, :]))
            for row, to in ((al_row, HL[:, :, D:D + HEADS]), (ar_row, erm[:, :, 0:HEADS])):
                link(dve.tensor_tensor(acc[:, :, :], Y[:, :, :], row[:, :].unsqueeze(1).to_broadcast([P, NB, D]), ALU.mult))
                link(dve.tensor_reduce(to, acc[:, :, :].rearrange("p b (h f) -> p b h f", h=HEADS), AX_X, ALU.add))
            dve.sem_inc(s_tab[0], 1)
            dve.memset(S[:, :, :, LW - 1:LW], 1.0).then_inc(s_tab[0], 1)

            def maxima(i):
                for g in range(SIDES):
                    if again(i):
                        dve.wait_ge(m.summed, GROUP * (SIDES * (i - 1) + g + 1))
                    for j in range(GROUP):
                        t = dve.tensor_scalar(NOT[:, g, j, :], iota[:, :], dloc[:, bass.ds(STEP * i + GROUP * g + j, 1)],
                                              -1.0, ALU.is_equal, ALU.add)
                    t.then_inc(m.onehot, 1)
                    regs = blocks_of(mybir.EngineType.DVE, block_of[0], STEP * i + GROUP * g)
                    for j in range(GROUP):
                        dve.wait_ge(m.summed, STEP * i + GROUP * g + j + 1)
                        dve.tensor_reduce(tmax[:, g, j, :], PS[:, g * GROUP + j, :].rearrange("p (h e) -> p h e", h=HEADS),
                                          AX_X, ALU.max).then_inc(s_mx, 1)
                    for j in range(GROUP):
                        at = elmax_flat[:, bass.ds(regs[j] * HEADS, HEADS)]
                        dve.wait_ge(s_mx, STEP * i + GROUP * g + j + 1)
                        after_tile_before(m, i, g, j)
                        dve.tensor_tensor(at, tmax[:, g, j, :], at, ALU.max).then_inc(m.added, 1)
            turns(dve, IT, maxima)
            dve.wait_ge(m.added, TILES)
            link(dve.tensor_scalar(elmax[:, :, :], elmax[:, :, :], -1.0e30, None, ALU.max))
            link(dve.tensor_tensor(small[:, :, :], elmax[:, :, :], erm[:, :, 0:HEADS], ALU.add))
            link(dve.tensor_scalar(elmax[:, :, :], small[:, :, :], SLOPE, None, ALU.mult))
            dve.tensor_tensor(erm[:, :, HEADS:2 * HEADS], elmax[:, :, :], small[:, :, :], ALU.max).then_inc(s_tab[0], 1)

            def messages(i):
                for g in range(SIDES):
                    onehots(w, i, g)
                    dve.wait_ge(w.load[g], 16 * (i + 1))
                    dve.wait_ge(w.looked, SIDES * i + g + 1)
                    looked = PS[:, 2 + g, 0:8 * GROUP].rearrange("p (j c) -> p j c", c=8)
                    dve.tensor_tensor(logit[:, g, :, :], looked[:, :, 0:HEADS], S[:, g, :, D:D + HEADS], ALU.add).then_inc(s_lg, 1)
                    dve.wait_ge(s_lg, SIDES * i + g + 1)
                    dve.scalar_tensor_tensor(slope[:, g, :, :].rearrange("p j h -> p (j h)"),
                                             logit[:, g, :, :].rearrange("p j h -> p (j h)"), SLOPE,
                                             logit[:, g, :, :].rearrange("p j h -> p (j h)"), ALU.mult, ALU.max).then_inc(s_lk, 1)
                    dve.wait_ge(s_lk, SIDES * i + g + 1)
                    dve.tensor_tensor(logit[:, g, :, :], slope[:, g, :, :], looked[:, :, HEADS:2 * HEADS], ALU.subtract).then_inc(s_lg2, 1)
                    dve.wait_ge(s_lg2, SIDES * i + g + 1)
                    dve.tensor_scalar(shift[:, g, :, :], logit[:, g, :, :], 0.0, None, ALU.min).then_inc(s_sh, 1)
                    dve.wait_ge(s_ex, SIDES * i + g + 1)
                    rows = S[:, g, :, 0:D].rearrange("p j (h f) -> p j h f", h=HEADS)
                    dve.tensor_tensor(rows, rows, S[:, g, :, D:D + HEADS].unsqueeze(3).to_broadcast([P, GROUP, HEADS, HF]),
                                      ALU.mult).then_inc(w.scaled, 1)
                    regs = blocks_of(mybir.EngineType.DVE, block_of[0], STEP * i + GROUP * g)
                    dve.wait_ge(w.summed, SIDES * i + g + 1)
                    for j in range(GROUP):
                        at = acc1_flat[:, bass.ds(regs[j] * LW, LW)]
                        after_tile_before(w, i, g, j)
                        dve.tensor_tensor(at, PS[:, 4 + 2 * g + j // 2, (j % 2) * 256:(j % 2) * 256 + LW], at,
                                          ALU.add).then_inc(w.added, 1)
            turns(dve, IT, messages)
            dve.wait_ge(w.added, TILES)
            link(dve.tensor_scalar(small[:, :, :], acc1[:, :, D:D + HEADS], 1e-20, None, ALU.max))
            link(dve.reciprocal(elmax[:, :, :], small[:, :, :]))
            for h in range(HEADS):
                at = acc1[:, :, h * HF:(h + 1) * HF]
                link(dve.tensor_tensor(acc[:, :, h * HF:(h + 1) * HF], at,
                                       elmax[:, :, h:h + 1].to_broadcast([P, NB, HF]), ALU.mult))
            link(dve.tensor_tensor(acc[:, :, :], acc[:, :, :], X3, ALU.add))
            link(dve.tensor_tensor(acc[:, :, :], acc[:, :, :], b1_row[:, :].unsqueeze(1).to_broadcast([P, NB, D]), ALU.add))
            link(dve.tensor_tensor(X3, X3, acc[:, :, :], ALU.add))
            nroot[0] += 1
            dve.tensor_scalar(dinv[:, :], acc1[:, :, LW - 1], 1.0, None, ALU.add).then_inc(s_var, 1)
            dve.wait_ge(s_std, nroot[0])
            link(dve.reciprocal(dinv[:, :], dinv[:, :]))
            norm(X3)
            dve.sem_inc(s_tab[1], 1)

            def aggregate(p):
                ahead(dve, IT, lambda i, g: onehots(p, i, g), lambda i, g: add_tiles(p, block_of[0], i, g))
                dve.wait_ge(p.added, TILES)

            link(dve.memset(acc[:, :, :], 0.0))
            aggregate(l2)
            five(1, acc_flat, take)
            dve.wait_ge(s_nd, 2 * (NB // 5))
            link(dve.tensor_tensor(Y[:, :, :], Y[:, :, :], b2_row[:, :].unsqueeze(1).to_broadcast([P, NB, D]), ALU.add))
            link(dve.tensor_tensor(X3, X3, Y[:, :, :], ALU.add))
            norm(X3)
            dve.tensor_tensor(Y[:, :, :], X3, dinv[:, :].unsqueeze(2).to_broadcast([P, NB, D]), ALU.mult).then_inc(s_tab[2], 1)
            dve.wait_ge(s_tab[2], 1)

            link(dve.tensor_copy(acc[:, :, :], Y[:, :, :]))
            aggregate(l3)
            dve.wait_ge(s_tabw[2], 16)
            five(2, acc_flat, take)
            dve.wait_ge(s_nd, 3 * (NB // 5))
            link(dve.tensor_tensor(Y[:, :, :], Y[:, :, :], dinv[:, :].unsqueeze(2).to_broadcast([P, NB, D]), ALU.mult))
            link(dve.tensor_tensor(Y[:, :, :], Y[:, :, :], b3_row[:, :].unsqueeze(1).to_broadcast([P, NB, D]), ALU.add))
            link(dve.tensor_scalar(Y[:, :, :], Y[:, :, :], 0.0, None, ALU.max))
            link(dve.tensor_tensor(X3, X3, Y[:, :, :], ALU.add))
            norm(X3)
            dve.sem_inc(s_fin, 1)


_INS = ['x', 'src', 'dst', 'edge_attr_128', 'L1_gnn_fc_w', 'L1_gnn_attn_l', 'L1_gnn_attn_r', 'L1_gnn_bias',
        'L2_gnn_W', 'L2_gnn_b', 'L3_gnn_W', 'L3_gnn_b']
_OUTS = [((3125, 128), 'float32')]


def kernel(**inputs):
    import numpy as _np
    import concourse.bacc as _bacc
    from concourse import mybir as _mybir
    from concourse.bass_utils import run_bass_kernel_spmd as _run

    nc = _bacc.Bacc("TRN2", target_bir_lowering=False, num_devices=1)
    arrays, args = {}, []
    for name in _INS:
        a = _np.ascontiguousarray(inputs[name])
        arrays[f"in_{name}_dram"] = a
        args.append(nc.dram_tensor(f"in_{name}_dram", a.shape, _mybir.dt.from_np(a.dtype), kind="ExternalInput").ap())
    for i, (shape, dtype) in enumerate(_OUTS):
        dt = _mybir.dt.from_np(_np.dtype(dtype))
        args.append(nc.dram_tensor(f"out_{i}_dram", shape, dt, kind="ExternalOutput").ap())
    gnn_program(nc, *args)
    r = _run(nc, [arrays], core_ids=[0])
    got = tuple(r.results[0][f"out_{i}_dram"] for i in range(len(_OUTS)))
    return got[0]
```

```python
from contextlib import ExitStack

import concourse.bass as bass
from concourse import mybir

ALU = mybir.AluOpType
ACT = mybir.ActivationFunctionType
AX_X = mybir.AxisListType.X
F32 = mybir.dt.float32
BF16 = mybir.dt.bfloat16
I32 = mybir.dt.int32
U32 = mybir.dt.uint32

P = 128
GROUP = 4
SIDES = 2
DEEP = 5
TURN = 10
ROW = 132
SRC, DST_IN_BLOCK, SRC_SLOT, SRC_IN_BLOCK = 128, 129, 130, 131
EPS = 1e-5
FAR = 2.0 ** 100
SLOPE = 0.2
NOWHERE = 255


def gnn_program(nc, x, src, dst, edge_attr, fc_w, attn_l, attn_r, bias1, w2, b2, w3, b3, out):
    N, D = x.shape
    E = src.shape[0]
    HEADS, HF = attn_l.shape
    NB = -(-N // P)
    FULL = N // P
    REST = N - FULL * P
    NP_ = NB * P
    EP = 125
    ET = E // EP
    assert EP * ET == E and D == P and HEADS * HF == D
    NGROUP = 5
    NRING = 5
    NIT = ET // (NGROUP * NRING)
    assert NIT * NGROUP * NRING == ET
    STEP = GROUP * TURN
    TILES = -(-((E + NB * P) // P) // STEP) * STEP
    IT = TILES // STEP
    GROUPS = TILES // GROUP
    SLOTS = TILES * P
    LW = 3 * HEADS + 1
    WIDE = ROW + 3 * HEADS
    PADS = 8
    assert TURN % SIDES == 0 and TURN % DEEP == 0 and TILES % PADS == 0

    record = nc.dram_tensor("record", [SLOTS, ROW], F32, kind="Internal").ap()
    record2 = nc.dram_tensor("record2", [SLOTS, ROW], F32, kind="Internal").ap()
    stash = nc.dram_tensor("stash", [TILES, P, ROW], F32, kind="Internal").ap()
    table1 = nc.dram_tensor("table1", [NP_, WIDE], F32, kind="Internal").ap()
    table2 = nc.dram_tensor("table2", [NP_, D], F32, kind="Internal").ap()
    table3 = nc.dram_tensor("table3", [NP_, D], F32, kind="Internal").ap()

    slots = record[0:SLOTS].rearrange("(k p) c -> p k c", p=P)
    slots2 = record2[0:SLOTS].rearrange("(k p) c -> p k c", p=P)
    stash_v = stash.rearrange("k p c -> p k c")
    edges = edge_attr.rearrange("(p t) f -> p t f", p=EP)

    with ExitStack() as ctx:
        def sb(name, shape, dt=F32):
            return ctx.enter_context(nc.sbuf_tensor(name, shape, dt))

        def sem(name):
            return ctx.enter_context(nc.semaphore(name))

        PS = ctx.enter_context(nc.psum_tensor("PS", [P, 8, 512], F32))

        SUMS = PS[:, :, :].rearrange("p k c -> p (k c)")[:, 0:NB * D]
        WSUMS = PS[:, 6, P:P + NB * LW]
        TURNED = PS[:, 7, 0:2 * P].bitcast(BF16)
        LOOKED = PS[:, 7, 2 * P:2 * P + 2 * GROUP * HEADS].rearrange("p (j c) -> p j c", j=GROUP)
        assert NB * D <= 6 * 512 + P and P + NB * LW <= 512

        lane_i = sb("lane_i", [P, 1], I32)
        lane = sb("lane", [P, 1])
        iota_i = sb("iota_i", [P, P], I32)
        iota = sb("iota", [P, P])
        ident = sb("ident", [P, P])
        before = sb("before", [P, P])
        ones = sb("ones", [P, P])
        far_id = sb("far_id", [P, P], BF16)
        iota_b = sb("iota_b", [P, P], BF16)
        ident_b = sb("ident_b", [P, P], BF16)
        zeros = sb("zeros", [P, 4 * P], BF16)
        parts_of = sb("parts_of", [3 * HEADS, 3])
        pick = sb("pick", [3 * HEADS, HEADS, P], BF16)
        tile_no_i = sb("tile_no_i", [P, GROUP], I32)
        tile_no = sb("tile_no", [P, GROUP])
        pad_i = sb("pad_i", [P, 1], I32)
        pad = sb("pad", [P, PADS, ROW])
        fcw = sb("fcw", [P, D])
        w2n = sb("w2n", [P, D])
        w2t = sb("w2t", [P, D])
        w3n = sb("w3n", [P, D])
        al_row = sb("al_row", [P, D])
        ar_row = sb("ar_row", [P, D])
        b1_row = sb("b1_row", [P, D])
        b2_row = sb("b2_row", [P, D])
        b3_row = sb("b3_row", [P, D])

        ends = [sb("dst_e", [EP, ET], I32), sb("src_e", [EP, ET], I32)]
        blk_i = sb("blk_i", [EP, ET], I32)
        blk = sb("blk", [EP, ET])
        end_f = sb("end_f", [EP, ET])
        pos = sb("pos", [EP, ET])
        shared2 = sb("shared2", [P, NB * ET])
        mask = shared2[0:EP, :].rearrange("p (b t) -> p b t", t=ET)
        shared = sb("shared", [P, NB * ET])
        run = shared[0:EP, :].rearrange("p (b t) -> p b t", t=ET)
        slot_d = sb("slot_d", [EP, ET], U32)
        meta = sb("meta", [EP, ET, 4], I32)
        upto = sb("upto", [EP, NB])
        cnt = sb("cnt", [EP, NB])
        base = sb("base", [EP, NB])
        tot_i = sb("tot_i", [P, NB], I32)
        ntile = sb("ntile", [P, NB])
        last = sb("last", [P, NB])
        first = sb("first", [P, NB])
        past = sb("past", [P, GROUP, NB])
        tblk = sb("tblk", [P, GROUP])
        tblk_i = [sb("tblk_d", [P, GROUP], I32), sb("tblk_s", [P, GROUP], I32)]
        block_of = [sb("block_of_d", [1, TILES], I32), sb("block_of_s", [1, TILES], I32)]

        NR = sb("NR", [EP, NRING, NGROUP, ROW])
        NX = sb("NX", [EP, NRING, NGROUP], U32)
        G = sb("G", [P, SIDES, GROUP, WIDE])
        OHT = sb("OHT", [P, SIDES, GROUP * P])
        NOT = sb("NOT", [P, SIDES, GROUP, P], BF16)
        IX = sb("IX", [P, SIDES, GROUP], U32)
        taken = [0]

        def ring(depth, width):
            lo, hi = taken[0], taken[0] + depth * GROUP * width
            taken[0] = hi
            return shared2[:, lo:hi].rearrange("p (g j f) -> p g j f", g=depth, f=width)
        S = ring(DEEP, ROW)
        OHF = ring(DEEP, P)
        R = ring(SIDES, ROW)
        M = ring(SIDES, ROW)
        M1 = ring(SIDES, D)
        OH = ring(SIDES, P)
        OHB = sb("OHB", [P, DEEP, GROUP, P], BF16)
        OHTB = sb("OHTB", [P, SIDES, GROUP * P], BF16)
        parts_t = sb("parts_t", [3 * HEADS, SIDES, GROUP * P], BF16)
        looked = sb("looked", [P, DEEP, GROUP, 2 * HEADS])
        logit = sb("logit", [P, SIDES, GROUP, HEADS])
        slope = sb("slope", [P, SIDES, GROUP, HEADS])
        shift = sb("shift", [P, SIDES, GROUP, HEADS])
        prob = sb("prob", [P, DEEP, GROUP, HEADS])
        left = sb("left", [P, SIDES, GROUP, HEADS])
        left2 = sb("left2", [P, SIDES, GROUP, HEADS])
        nought = sb("nought", [P, GROUP, HEADS])
        probs = sb("probs", [P, DEEP, GROUP, LW], BF16)
        tmax = sb("tmax", [P, SIDES, GROUP, HEADS])
        src_of = sb("src_of", [P, TILES], U32)
        dloc = sb("dloc", [P, TILES])

        X = sb("X", [P, NB * D])
        X3 = X[:, :].rearrange("p (b f) -> p b f", f=D)
        o1, o3 = NB * D, NB * (D + WIDE)
        Y = shared[:, 0:o1].rearrange("p (b f) -> p b f", f=D)
        acc = sb("acc", [P, NB, D])
        acc_flat = acc[:, :, :].rearrange("p b f -> p (b f)")
        HL = shared[:, o1:o3].rearrange("p (b f) -> p b f", f=WIDE)
        acc1 = sb("acc1", [P, NB, LW])
        erm = sb("erm", [P, NB, 2 * HEADS])
        erm_b = sb("erm_b", [P, NB, 3, 2 * HEADS], BF16)
        erm_bflat = erm_b[:, :, :, :].rearrange("p b k f -> p (b k f)")
        rest = sb("rest", [P, NB, 2 * HEADS])
        elmax = sb("elmax", [P, NB, HEADS])
        elmax_flat = elmax[:, :, :].rearrange("p b f -> p (b f)")
        stage = sb("stage", [P, 5, D])
        xt = sb("xt", [P, 5 * P])
        nsum = sb("nsum", [P, NB])
        nvar = sb("nvar", [P, NB])
        rstd = sb("rstd", [P, NB])
        dinv = sb("dinv", [P, NB])
        small = sb("small", [P, NB, HEADS])

        s_w = sem("weights_loaded")
        s_x = sem("x_loaded")
        s_ends = sem("ends_loaded")
        s_iota = sem("iotas_made")
        s_dv = sem("vector_chain")
        s_gate = sem("pool_gate")
        s_pad = sem("pad_made")
        s_blank = sem("record_blank")
        s_blank2 = sem("record2_blank")
        s_cnt = sem("counts_made")
        s_tot = sem("counts_summed")
        s_tb = sem("tile_blocks_made")
        s_tbl = sem("tile_blocks_laid")
        s_clear = sem("x_padding_cleared")
        s_w2 = sem("w2_turned")
        s_nload = [sem(f"edges_loaded{g}") for g in range(NRING)]
        s_nmeta = sem("meta_filled")
        s_nput = [sem(f"edges_put{g}") for g in range(NRING)]

        class Sems:
            def __init__(self, name):
                self.load = [sem(f"{name}_load{g}") for g in range(SIDES)]
                self.gather = [sem(f"{name}_gathered{g}") for g in range(SIDES)]
                self.put = [sem(f"{name}_put{g}") for g in range(SIDES)]
                self.ix = sem(f"{name}_indices")
                self.onehot = sem(f"{name}_onehot")
                self.turned = sem(f"{name}_turned")
                self.onehot_t = sem(f"{name}_onehot_t")
                self.looked = sem(f"{name}_looked_up")
                self.scaled = sem(f"{name}_scaled")
                self.summed = sem(f"{name}_summed")
                self.added = sem(f"{name}_added")

        a = Sems("a")
        c = Sems("c")
        m = Sems("m")
        w = Sems("w")
        l2, l3 = Sems("l2"), Sems("l3")
        s_m2 = sem("a_source_messages")
        load_c = [sem(f"c_loaded{g}") for g in range(DEEP)]
        load_w = [sem(f"w_loaded{g}") for g in range(DEEP)]
        s_mt = sem("m_parts_turned")
        s_mc = sem("m_parts_copied")
        s_mx = sem("m_tile_max")
        s_of = sem("w_onehot_float")
        s_lc = sem("w_looked_up_taken")
        s_pp = [sem(f"w_weight_part{n}") for n in range(5)]
        s_clr = sem("sums_cleared")
        s_tot_c, s_tot_w, s_tot_2, s_tot_3 = [sem(f"{n}_sums_complete") for n in "cw23"]
        s_lg = sem("w_logit")
        s_lk = sem("w_leaky")
        s_lg2 = sem("w_less_maximum")
        s_sh = sem("w_shifted")
        s_ex = sem("w_exp")

        s_half = sem("second_half_taken")
        s_nx = sem("nodes_ready")
        s_nt = sem("nodes_turned")
        s_ntc = sem("nodes_turned_copied")
        s_nm = sem("nodes_multiplied")
        s_nd = sem("nodes_taken")
        s_var = sem("variance_ready")
        s_std = sem("deviation_ready")
        s_tab = [sem(f"table{n}_ready") for n in range(3)]
        s_tabw = [sem(f"table{n}_written") for n in range(3)]
        s_fin = sem("result_ready")
        s_out = sem("result_written")

        HALF = NB // 2 * D
        block = ctx.enter_context(nc.Block())

        def again(i):
            return not (isinstance(i, int) and i == 0)

        def turns(eng, n, body):
            body(0)
            with eng.Fori(1, n) as i:
                body(i)

        def pipeline(eng, *stages):
            def at(i, q):
                for body, lead in stages:
                    ii, qq = i + (q + lead) // TURN, (q + lead) % TURN
                    if not isinstance(ii, int) or 0 <= ii < IT:
                        body(ii, qq)
            for q in range(TURN - max(lead for _, lead in stages), TURN):
                at(-1, q)
            for q in range(TURN):
                at(0, q)
            with eng.Fori(1, IT - 1) as i:
                for q in range(TURN):
                    at(i, q)
            for q in range(TURN):
                at(IT - 1, q)

        def group(i, q):
            return TURN * i + q

        def use(i, q, ring):
            return TURN // ring * i + q // ring

        def used(i, q, ring):
            return not isinstance(i, int) or group(i, q) >= ring

        def freed(eng, sem_, i, q, ring, per=1):
            if used(i, q, ring):
                eng.wait_ge(sem_, per * (group(i, q) - ring + 1))

        def blocks_of(eng_type, table, t0):
            _, regs = nc.values_load_multi_w_load_instructions(
                table[0:1, bass.ds(t0, GROUP)], engines=[eng_type], min_val=0, max_val=NB - 1,
                skip_runtime_bounds_check_because="the table is clamped to the last block")
            return regs

        @block.sync
        def _(sp):
            for e, given in zip(ends, (dst, src)):
                sp.dma_start(e[:, :], given.rearrange("(p t) -> p t", p=EP)).then_inc(s_ends, 16)
            sp.dma_start(X3[:, 0:FULL, :], x[0:FULL * P, :].rearrange("(b p) f -> p b f", p=P)).then_inc(s_x, 16)
            sp.wait_ge(s_clear, 1)
            sp.dma_start(X3[0:REST, FULL, :], x[FULL * P:N, :]).then_inc(s_x, 16)
            for t, given in ((fcw, fc_w), (w2n, w2), (w3n, w3)):
                sp.dma_start(t[:, :], given).then_inc(s_w, 16)
            for t, given in ((al_row, attn_l.rearrange("h f -> (h f)")), (ar_row, attn_r.rearrange("h f -> (h f)")),
                             (b1_row, bias1), (b2_row, b2), (b3_row, b3)):
                sp.dma_start(t[:, :], given.partition_broadcast(P)).then_inc(s_w, 16)
            sp.wait_ge(s_pad, 1)
            for rec, s in ((slots, s_blank), (slots2, s_blank2)):
                with sp.Fori(0, TILES // PADS) as i:
                    sp.dma_start(rec[:, bass.ds(PADS * i, PADS), :], pad[:, :, :]).then_inc(s, 16)
            for n in range(2):
                sp.wait_ge(s_tb, n + 1)
                sp.dma_start(block_of[n][0:1, :].rearrange("a (p q) -> a p q", q=GROUP),
                             tblk_i[n][0:TILES // GROUP, :]).then_inc(s_tbl, 16)

            def load_edges(i):
                for g in range(NRING):
                    if again(i):
                        sp.wait_ge(s_nput[g], 16 * NGROUP * i)
                    sp.dma_start(NR[:, g, :, 0:D],
                                 edges[:, bass.ds((i * NRING + g) * NGROUP, NGROUP), :]).then_inc(s_nload[g], 16)
            turns(sp, NIT, load_edges)
            for g in range(NRING):
                sp.wait_ge(s_nput[g], 16 * NGROUP * NIT)

            def tiles(i, q):
                return bass.ds(GROUP * group(i, q), GROUP)

            def load_records(i, q):
                g = q % SIDES
                freed(sp, s_m2, i, q, SIDES)
                sp.dma_start(R[:, g, :, :], slots[:, tiles(i, q), :]).then_inc(a.load[g], 16)
            pipeline(sp, (load_records, 0))

            for g in range(SIDES):
                sp.wait_ge(a.put[g], 16 * TILES // SIDES)

            def load_records2(i, q):
                freed(sp, c.summed, i, q, DEEP)
                sp.dma_start(S[:, q % DEEP, :, :], slots2[:, tiles(i, q), :]).then_inc(load_c[q % DEEP], 16)
            pipeline(sp, (load_records2, 0))

            sp.wait_ge(s_tab[0], 1)
            sp.dma_start(table1.rearrange("(b p) c -> p b c", p=P), HL[:, :, :]).then_inc(s_tabw[0], 16)

            def keep_rows(i, q):
                g = q % SIDES
                sp.wait_ge(m.gather[g], 16 * GROUP * (use(i, q, SIDES) + 1))
                sp.dma_start(stash_v[:, tiles(i, q), :], G[:, g, :, 0:ROW]).then_inc(m.put[g], 16)
            pipeline(sp, (keep_rows, 0))
            for g in range(SIDES):
                sp.wait_ge(m.put[g], 16 * GROUPS // SIDES)

            def load_rows(i, q):
                freed(sp, w.summed, i, q, DEEP)
                sp.dma_start(S[:, q % DEEP, :, :], stash_v[:, tiles(i, q), :]).then_inc(load_w[q % DEEP], 16)
            pipeline(sp, (load_rows, 0))

            sp.wait_ge(s_tab[1], 1)
            sp.dma_start(table2.rearrange("(b p) c -> p b c", p=P), X3).then_inc(s_tabw[1], 16)
            sp.wait_ge(s_tab[2], 1)
            sp.dma_start(table3.rearrange("(b p) c -> p b c", p=P), Y[:, :, :]).then_inc(s_tabw[2], 16)
            sp.wait_ge(s_fin, 1)
            sp.dma_start(out[0:FULL * P, :].rearrange("(b p) f -> p b f", p=P), X3[:, 0:FULL, :]).then_inc(s_out, 16)
            sp.dma_start(out[FULL * P:N, :], X3[0:REST, FULL, :]).then_inc(s_out, 16)
            sp.wait_ge(s_out, 32)
            sp.wait_ge(s_blank, 16 * (TILES // PADS))
            sp.wait_ge(s_blank2, 16 * (TILES // PADS))
            for n in range(3):
                sp.wait_ge(s_tabw[n], 16)

        @block.gpsimd
        def _(pool):
            def row_index(ap):
                return bass.IndirectOffsetOnAxis(ap, 0)

            pool.iota(iota_i[:, :], [[1, P]], base=0, channel_multiplier=0).then_inc(s_iota, 1)
            pool.iota(lane_i[:, :], [[0, 1]], base=0, channel_multiplier=1).then_inc(s_iota, 1)
            pool.iota(tile_no_i[:, :], [[1, GROUP]], base=0, channel_multiplier=GROUP).then_inc(s_iota, 1)
            pool.iota(pad_i[:, :], [[0, 1]], base=SLOTS, channel_multiplier=0).then_inc(s_iota, 1)
            pool.memset(pad[:, :, :], 0.0).then_inc(s_iota, 1)

            pool.wait_ge(s_blank, 16 * (TILES // PADS))

            def put_edges(i):
                for g in range(NRING):
                    pool.wait_ge(s_nload[g], 16 * (i + 1))
                    pool.wait_ge(s_nmeta, NRING * i + g + 1)
                    pool.sem_inc(s_gate, 1)
                    for j in range(NGROUP):
                        pool.indirect_dma_start(record[:, :], row_index(NX[:, g, j:j + 1]), NR[:, g, j, :],
                                                None).then_inc(s_nput[g], 16)
            turns(pool, NIT, put_edges)
            pool.wait_ge(s_blank2, 16 * (TILES // PADS))

            def gather_x(i, q):
                g = q % SIDES
                pool.wait_ge(a.load[g], 16 * (use(i, q, SIDES) + 1))
                freed(pool, a.scaled, i, q, SIDES)
                pool.sem_inc(s_gate, 1)
                for j in range(GROUP):
                    pool.indirect_dma_start(G[:, g, j, 0:D], None, x[:, :],
                                            row_index(R[:, g, j, SRC:SRC + 1].bitcast(U32))).then_inc(a.gather[g], 16)

            def put_messages(i, q):
                g = q % SIDES
                pool.wait_ge(s_m2, group(i, q) + 1)
                pool.sem_inc(s_gate, 1)
                for j in range(GROUP):
                    pool.indirect_dma_start(record2[:, :], row_index(IX[:, g, j:j + 1]),
                                            M[:, g, j, :], None, bounds_check=SLOTS - 1,
                                            oob_is_err=False).then_inc(a.put[g], 16)
            pipeline(pool, (gather_x, 1), (put_messages, 0))

            def gather_rows(p, table, width, free, per):
                def step(i, q):
                    g = q % SIDES
                    if used(i, q, SIDES):
                        pool.wait_ge(p.gather[g], 16 * GROUP * use(i, q, SIDES))
                        pool.sem_inc(s_gate, 1)
                    pool.tensor_copy(IX[:, g, :], src_of[:, bass.ds(GROUP * group(i, q), GROUP)]).then_inc(p.ix, 1)
                    pool.wait_ge(p.ix, group(i, q) + 1)
                    freed(pool, free, i, q, SIDES, per)
                    if p is m and used(i, q, SIDES):
                        pool.wait_ge(m.put[g], 16 * use(i, q, SIDES))
                    pool.sem_inc(s_gate, 1)
                    for j in range(GROUP):
                        pool.indirect_dma_start(G[:, g, j, 0:width], None, table[:, :],
                                                row_index(IX[:, g, j:j + 1])).then_inc(p.gather[g], 16)
                pipeline(pool, (step, 0))

            for g in range(SIDES):
                pool.wait_ge(a.put[g], 16 * TILES // SIDES)
            pool.wait_ge(s_tabw[0], 16)
            gather_rows(m, table1, WIDE, m.summed, GROUP)

            def split(i, q):
                g, d = q % SIDES, q % DEEP
                n = group(i, q) + 1
                pool.wait_ge(s_ex, n)
                freed(pool, w.summed, i, q, DEEP)
                pool.sem_inc(s_gate, 1)
                pool.tensor_tensor(probs[:, d, :, 0:HEADS], prob[:, d, :, :], nought[:, :, :], ALU.add).then_inc(s_pp[0], 1)
                pool.wait_ge(s_pp[0], n)
                pool.tensor_tensor(left[:, g, :, :], prob[:, d, :, :], probs[:, d, :, 0:HEADS], ALU.subtract).then_inc(s_pp[1], 1)
                pool.wait_ge(s_pp[1], n)
                pool.tensor_tensor(probs[:, d, :, HEADS:2 * HEADS], left[:, g, :, :], nought[:, :, :], ALU.add).then_inc(s_pp[2], 1)
                pool.wait_ge(s_pp[2], n)
                pool.tensor_tensor(left2[:, g, :, :], left[:, g, :, :], probs[:, d, :, HEADS:2 * HEADS], ALU.subtract).then_inc(s_pp[3], 1)
                pool.wait_ge(s_pp[3], n)
                pool.tensor_tensor(probs[:, d, :, 2 * HEADS:3 * HEADS], left2[:, g, :, :], nought[:, :, :], ALU.add).then_inc(s_pp[4], 1)
            pipeline(pool, (split, 0))

            for g in range(SIDES):
                pool.wait_ge(m.put[g], 16 * GROUPS // SIDES)
            pool.wait_ge(s_tabw[1], 16)
            gather_rows(l2, table2, D, l2.summed, 1)
            pool.wait_ge(s_tabw[2], 16)
            gather_rows(l3, table3, D, l3.summed, 1)

        @block.tensor
        def _(pe):
            for n in range(2):
                pe.wait_ge(s_cnt, n + 1)
                pe.matmul(PS[0:EP, 0, 0:NB], before[0:EP, 0:EP], cnt[:, :], start=True, stop=True)
                pe.matmul(PS[:, 1, 0:NB], ones[0:EP, :], cnt[:, :], start=True, stop=True).then_inc(s_tot, 1)
            pe.wait_ge(s_w, 16 * 8)
            pe.transpose(PS[:, 7, 0:P], w2n[:, :], ident[:, :]).then_inc(s_w2, 1)

            PE = mybir.EngineType.PE

            pe.wait_ge(s_tbl, 32)
            pe.wait_ge(s_x, 32)

            def look_up(i, q):
                g, n = q % SIDES, group(i, q)
                pe.wait_ge(a.onehot, n + 1)
                freed(pe, a.onehot_t, i, q, SIDES)
                for j in range(GROUP):
                    t = pe.transpose(PS[:, g, j * P:(j + 1) * P], OH[:, g, j, :], ident[:, :])
                t.then_inc(a.turned, 1)
                regs = blocks_of(PE, block_of[0], GROUP * n)
                pe.wait_ge(a.onehot_t, n + 1)
                freed(pe, s_m2, i, q, SIDES)
                for j in range(GROUP):
                    t = pe.matmul(PS[:, 2 + g, j * P:(j + 1) * P], OHT[:, g, j * P:(j + 1) * P],
                                  X[:, bass.ds(regs[j] * D, D)], start=True, stop=True)
                t.then_inc(a.looked, 1)

            def sum_a(i, q):
                g, n = q % SIDES, group(i, q)
                pe.wait_ge(a.scaled, n + 1)
                freed(pe, a.added, i, q, SIDES, GROUP)
                for j in range(GROUP):
                    t = pe.matmul(PS[:, 4 + g, j * P:(j + 1) * P], OH[:, g, j, :], M1[:, g, j, :], start=True, stop=True)
                t.then_inc(a.summed, 1)
            pipeline(pe, (look_up, 0), (sum_a, 0))

            def clear_sums():
                for b in range(7):
                    t = pe.matmul(PS[:, b, :], zeros[:, 0:P], zeros[:, :], start=True, stop=True)

            def sum_into_blocks(p, table, onehot, rows, arrived, per, ring):
                def step(i, q):
                    n = group(i, q)
                    regs = blocks_of(PE, table, GROUP * n)
                    pe.wait_ge(p.onehot, n + 1)
                    pe.wait_ge(arrived[q % ring], per * (use(i, q, ring) + 1))
                    for j in range(GROUP):
                        t = pe.matmul(SUMS[:, bass.ds(regs[j] * D, D)], onehot[:, q % DEEP, j, :],
                                      rows[:, q % ring, j, 0:D], start=False, stop=True, skip_group_check=True)
                    t.then_inc(p.summed, 1)
                pipeline(pe, (step, 0))

            pe.wait_ge(a.added, TILES)
            clear_sums()
            sum_into_blocks(c, block_of[1], OHF, S, load_c, 16, DEEP)

            def five(weights, turn):
                with pe.Fori(0, NB // 5) as i:
                    n = i + turn * (NB // 5)
                    pe.wait_ge(s_nx, n + 1)
                    for b in range(5):
                        t = pe.transpose(PS[:, b // 4, (b % 4) * P:(b % 4 + 1) * P], stage[:, b, :], ident[:, :])
                    t.then_inc(s_nt, 1)
                    pe.wait_ge(s_ntc, n + 1)
                    for b in range(5):
                        t = pe.matmul(PS[:, 2 + b // 4, (b % 4) * P:(b % 4 + 1) * P], xt[:, b * P:(b + 1) * P],
                                      weights[:, :], start=True, stop=True)
                    t.then_inc(s_nm, 1)
            pe.wait_ge(s_tot_c, 1)
            five(fcw, 0)

            def turn_parts(i, q):
                g, n = q % SIDES, group(i, q)
                pe.wait_ge(m.gather[g], 16 * GROUP * (use(i, q, SIDES) + 1))
                freed(pe, s_mc, i, q, SIDES)
                for j in range(GROUP):
                    t = pe.transpose(PS[0:3 * HEADS, 6 + g, j * P:(j + 1) * P], G[:, g, j, ROW:WIDE], ident[:, :])
                t.then_inc(s_mt, 1)

            def maxima(i, q):
                g, n = q % SIDES, group(i, q)
                pe.wait_ge(m.onehot, n + 1)
                pe.wait_ge(s_mc, n + 1)
                for j in range(GROUP):
                    if j % 2 == 0:
                        if used(i, q, 1):
                            pe.wait_ge(s_mx, 2 * n - 1 + j // 2)
                    for h in range(HEADS):
                        at = PS[:, j, h * P:(h + 1) * P]
                        pe.matmul(at, NOT[:, g, j, :], far_id[:, :], start=True, stop=False)
                        t = pe.matmul(at, pick[:, h, :], parts_t[:, g, j * P:(j + 1) * P], start=False, stop=True)
                    t.then_inc(m.summed, 1)
            pe.wait_ge(s_nd, NB // 5)
            pipeline(pe, (turn_parts, 0), (maxima, 0))

            pe.wait_ge(s_tab[0], 2)
            clear_sums()

            def turn_onehot(i, q):
                pe.wait_ge(w.onehot, group(i, q) + 1)
                freed(pe, s_lc, i, q, 1)
                for j in range(GROUP):
                    t = pe.transpose(TURNED[:, j * P:(j + 1) * P], OHB[:, q % DEEP, j, :], ident_b[:, :])
                t.then_inc(w.turned, 1)

            def look_up_logits(i, q):
                g, n = q % SIDES, group(i, q)
                regs = blocks_of(PE, block_of[0], GROUP * n)
                pe.wait_ge(w.onehot_t, n + 1)
                for j in range(GROUP):
                    for k in range(3):
                        t = pe.matmul(LOOKED[:, j, :], OHTB[:, g, j * P:(j + 1) * P],
                                      erm_bflat[:, bass.ds(regs[j] * (6 * HEADS) + 2 * HEADS * k, 2 * HEADS)],
                                      start=(k == 0), stop=(k == 2))
                t.then_inc(w.looked, 1)

            def sum_messages(tiles, last):
                def step(i, q):
                    d, n = q % DEEP, group(i, q)
                    _, regs = nc.values_load_multi_w_load_instructions(
                        block_of[0][0:1, bass.ds(GROUP * n + tiles[0], len(tiles))], engines=[PE], min_val=0,
                        max_val=NB - 1, skip_runtime_bounds_check_because="the table is clamped to the last block")
                    if not last:
                        pe.wait_ge(s_of, n + 1)
                        pe.wait_ge(w.scaled, n + 1)
                        pe.wait_ge(s_pp[4], n + 1)
                    for j, r in zip(tiles, regs):
                        pe.matmul(SUMS[:, bass.ds(r * D, D)], OHF[:, d, j, :], S[:, d, j, 0:D],
                                  start=False, stop=True, skip_group_check=True)
                        t = pe.matmul(WSUMS[:, bass.ds(r * LW, LW)], OHB[:, d, j, :], probs[:, d, j, :],
                                      start=False, stop=True, skip_group_check=True)
                    if last:
                        t.then_inc(w.summed, 1)
                return step
            pipeline(pe, (turn_onehot, 2), (sum_messages([0, 1], False), 0), (look_up_logits, 2),
                     (sum_messages([2, 3], True), 0))

            pe.wait_ge(s_tot_w, 1)
            clear_sums()
            sum_into_blocks(l2, block_of[0], OHF, G, l2.gather, 16 * GROUP, SIDES)
            pe.wait_ge(s_tot_2, 1)
            five(w2t, 1)
            pe.wait_ge(s_nd, 2 * (NB // 5))
            clear_sums()
            sum_into_blocks(l3, block_of[0], OHF, G, l3.gather, 16 * GROUP, SIDES)
            pe.wait_ge(s_tot_3, 1)
            five(w3n, 2)

        @block.scalar
        def _(act):
            def copy_turned(i, q):
                g, n = q % SIDES, group(i, q)
                act.wait_ge(a.turned, n + 1)
                freed(act, a.looked, i, q, SIDES)
                act.activation(OHT[:, g, :], PS[:, g, :], ACT.Copy).then_inc(a.onehot_t, 1)

            def five(turn):
                with act.Fori(0, NB // 5) as i:
                    n = i + turn * (NB // 5)
                    act.wait_ge(s_nt, n + 1)
                    act.activation(xt[:, 0:4 * P], PS[:, 0, :], ACT.Copy)
                    act.activation(xt[:, 4 * P:5 * P], PS[:, 1, 0:P], ACT.Copy).then_inc(s_ntc, 1)

            def root(n):
                act.wait_ge(s_var, n)
                act.activation(nvar[:, :], nvar[:, :], ACT.Sqrt).then_inc(s_std, 1)

            def take_sums(total, left):
                act.wait_ge(total, GROUPS)
                act.activation(acc_flat[:, HALF:NB * D], SUMS[:, HALF:NB * D], ACT.Copy).then_inc(left, 1)

            pipeline(act, (copy_turned, 0))
            root(1)
            five(0)

            def copy_parts(i, q):
                g, n = q % SIDES, group(i, q)
                act.wait_ge(s_mt, n + 1)
                freed(act, m.summed, i, q, SIDES, GROUP)
                act.activation(parts_t[:, g, :], PS[0:3 * HEADS, 6 + g, :], ACT.Copy).then_inc(s_mc, 1)
            pipeline(act, (copy_parts, 0))

            def copy_onehots(i, q):
                g, d, n = q % SIDES, q % DEEP, group(i, q)
                act.wait_ge(w.turned, n + 1)
                freed(act, w.looked, i, q, SIDES)
                act.activation(OHTB[:, g, :], TURNED, ACT.Copy).then_inc(w.onehot_t, 1)
                freed(act, w.summed, i, q, DEEP)
                act.activation(OHF[:, d, :, :], OHB[:, d, :, :], ACT.Copy).then_inc(s_of, 1)

            def weights(i, q):
                act.wait_ge(s_sh, group(i, q) + 1)
                freed(act, w.summed, i, q, DEEP)
                act.activation(prob[:, q % DEEP, :, :], shift[:, q % SIDES, :, :], ACT.Exp).then_inc(s_ex, 1)
            pipeline(act, (copy_onehots, 2), (weights, 1))
            act.wait_ge(s_var, 2)
            act.activation(dinv[:, :], dinv[:, :], ACT.Sqrt).then_inc(s_std, 1)
            root(3)
            take_sums(l2.summed, s_half)
            five(1)
            root(4)
            take_sums(l3.summed, s_half)
            five(2)
            root(5)

        @block.vector
        def _(dve):
            done = [0]

            def link(ins):
                done[0] += 1
                ins.then_inc(s_dv, 1)
                dve.wait_ge(s_dv, done[0])

            dve.memset(X3[:, FULL, :], 0.0).then_inc(s_clear, 1)
            dve.wait_ge(s_iota, 5)
            link(dve.tensor_copy(iota[:, :], iota_i[:, :]))
            link(dve.tensor_copy(lane[:, :], lane_i[:, :]))
            link(dve.tensor_copy(tile_no[:, :], tile_no_i[:, :]))
            link(dve.tensor_scalar(ident[:, :], iota[:, :], lane[:, 0:1], None, ALU.is_equal))
            dve.tensor_scalar(before[:, :], iota[:, :], lane[:, 0:1], None, ALU.is_gt)
            dve.memset(ones[:, :], 1.0)
            dve.tensor_copy(iota_b[:, :], iota_i[:, :])
            dve.tensor_copy(ident_b[:, :], ident[:, :])
            dve.memset(zeros[:, :], 0.0)
            dve.memset(nought[:, :, :], 0.0)
            dve.memset(probs[:, :, :, LW - 1:LW], 1.0)
            link(dve.tensor_scalar(parts_of[:, 0:1], lane[0:3 * HEADS, :], float(HEADS), None, ALU.is_ge))
            link(dve.tensor_scalar(parts_of[:, 1:2], lane[0:3 * HEADS, :], float(2 * HEADS), None, ALU.is_ge))
            link(dve.tensor_tensor(parts_of[:, 0:1], parts_of[:, 0:1], parts_of[:, 1:2], ALU.add))
            link(dve.scalar_tensor_tensor(parts_of[:, 2:3], parts_of[:, 0:1], -float(HEADS), lane[0:3 * HEADS, :],
                                          ALU.mult, ALU.add))
            for h in range(HEADS):
                dve.tensor_scalar(pick[:, h, :], parts_of[:, 2:3].to_broadcast([3 * HEADS, P]), float(h), None, ALU.is_equal)
            dve.tensor_scalar(far_id[:, :], ident[:, :], FAR, None, ALU.mult)
            pad_int = pad[:, :, :].bitcast(I32)
            for col in (DST_IN_BLOCK, SRC_IN_BLOCK):
                link(dve.tensor_scalar(pad_int[:, :, col], pad_int[:, :, 0], float(NOWHERE), None, ALU.add))
            dve.tensor_copy(pad_int[:, :, SRC_SLOT], pad_i[:, 0:1].to_broadcast([P, PADS])).then_inc(s_pad, 1)

            dve.wait_ge(s_ends, 32)
            for n in range(2):
                link(dve.tensor_copy(end_f[:, :], ends[n][:, :]))
                link(dve.tensor_scalar(blk_i[:, :], ends[n][:, :], 7, None, ALU.arith_shift_right))
                link(dve.tensor_copy(blk[:, :], blk_i[:, :]))
                col = (DST_IN_BLOCK, SRC_IN_BLOCK)[n] - D
                link(dve.scalar_tensor_tensor(meta[:, :, col], blk[:, :], -float(P), end_f[:, :], ALU.mult, ALU.add))
                if n == 1:
                    link(dve.tensor_copy(meta[:, :, SRC - D], ends[1][:, :]))
                link(dve.tensor_tensor(mask[:, :, :], blk[:, :].unsqueeze(1).to_broadcast([EP, NB, ET]),
                                       iota[0:EP, 0:NB].unsqueeze(2).to_broadcast([EP, NB, ET]), ALU.is_equal))
                flat_run = shared[0:EP, :]
                flat_mask = shared2[0:EP, :]
                link(dve.tensor_tensor_scan(flat_run, flat_mask, flat_mask, 0.0, ALU.add, ALU.max))
                link(dve.tensor_copy(upto[:, :], run[:, :, ET - 1]))
                link(dve.tensor_copy(cnt[:, 0:1], upto[:, 0:1]))
                dve.tensor_tensor(cnt[:, 1:NB], upto[:, 1:NB], upto[:, 0:NB - 1], ALU.subtract).then_inc(s_cnt, 1)
                dve.wait_ge(s_tot, n + 1)
                link(dve.tensor_scalar(tot_i[:, :], PS[:, 1, 0:NB], float(P - 1), None, ALU.add))
                link(dve.tensor_scalar(tot_i[:, :], tot_i[:, :], 7, None, ALU.arith_shift_right))
                link(dve.tensor_scalar(ntile[:, :], tot_i[:, :], 1.0, None, ALU.max))
                link(dve.tensor_tensor_scan(last[:, :], ntile[:, :], ntile[:, :], 0.0, ALU.add, ALU.max))
                link(dve.tensor_tensor(first[:, :], last[:, :], ntile[:, :], ALU.subtract))
                link(dve.scalar_tensor_tensor(base[:, :], first[0:EP, :], float(P), PS[0:EP, 0, 0:NB],
                                              ALU.mult, ALU.add))
                link(dve.tensor_tensor(base[:, :], base[:, :], upto[:, :], ALU.subtract))
                link(dve.tensor_tensor(base[:, :], base[:, :], cnt[:, :], ALU.add))
                link(dve.tensor_scalar(base[:, :], base[:, :], -1.0, None, ALU.add))
                link(dve.tensor_tensor(run[:, :, :], run[:, :, :], base[:, :].unsqueeze(2).to_broadcast([EP, NB, ET]),
                                       ALU.add))
                link(dve.tensor_tensor(run[:, :, :], run[:, :, :], mask[:, :, :], ALU.mult))
                link(dve.tensor_reduce(pos[:, :], run[:, :, :].rearrange("p b t -> p t b"), AX_X, ALU.add))
                if n == 0:
                    link(dve.tensor_copy(slot_d[:, :], pos[:, :]))
                else:
                    link(dve.tensor_copy(meta[:, :, SRC_SLOT - D], pos[:, :]))
                link(dve.tensor_tensor(past[:, :, :], tile_no[:, :].unsqueeze(2).to_broadcast([P, GROUP, NB]),
                                       last[:, :].unsqueeze(1).to_broadcast([P, GROUP, NB]), ALU.is_ge))
                link(dve.tensor_reduce(tblk[:, :], past[:, :, :], AX_X, ALU.add))
                dve.tensor_scalar(tblk_i[n][:, :], tblk[:, :], float(NB - 1), None, ALU.min).then_inc(s_tb, 1)

            def fill_meta(i):
                for g in range(NRING):
                    if again(i):
                        dve.wait_ge(s_nput[g], 16 * NGROUP * i)
                    t0 = (i * NRING + g) * NGROUP
                    dve.tensor_copy(NR[:, g, :, D:ROW].bitcast(I32), meta[:, bass.ds(t0, NGROUP), :])
                    dve.tensor_copy(NX[:, g, :], slot_d[:, bass.ds(t0, NGROUP)]).then_inc(s_nmeta, 1)
            turns(dve, NIT, fill_meta)

            dve.wait_ge(s_w2, 1)
            link(dve.tensor_copy(w2t[:, :], PS[:, 7, 0:P]))
            link(dve.memset(acc[:, :, :], 0.0))
            link(dve.memset(elmax[:, :, :], -3.0e38))
            dve.wait_ge(s_tbl, 32)
            dve.wait_ge(s_x, 32)

            DVE = mybir.EngineType.DVE

            def after_tile_before(p, i, q, j):
                if used(i, q, 1) or j > 0:
                    dve.wait_ge(p.added, GROUP * group(i, q) + j)

            def onehots_a(i, q):
                g, n = q % SIDES, group(i, q)
                Ri = R[:, g, :, :].bitcast(I32)
                dve.wait_ge(a.load[g], 16 * (use(i, q, SIDES) + 1))
                freed(dve, a.summed, i, q, SIDES)
                for j in range(GROUP):
                    t = dve.tensor_scalar(OH[:, g, j, :], iota[:, :], Ri[:, j, DST_IN_BLOCK:DST_IN_BLOCK + 1],
                                          None, ALU.is_equal)
                t.then_inc(a.onehot, 1)
                dve.tensor_copy(src_of[:, bass.ds(GROUP * n, GROUP)], Ri[:, :, SRC])
                dve.tensor_copy(dloc[:, bass.ds(GROUP * n, GROUP)], Ri[:, :, DST_IN_BLOCK])

            def layer0(i, q):
                g, n = q % SIDES, group(i, q)
                Ri = R[:, g, :, :].bitcast(I32)
                dve.wait_ge(a.gather[g], 16 * GROUP * (use(i, q, SIDES) + 1))
                dve.tensor_tensor(M1[:, g, :, :], G[:, g, :, 0:D], R[:, g, :, 0:D], ALU.mult).then_inc(a.scaled, 1)
                if used(i, q, SIDES):
                    dve.wait_ge(a.put[g], 16 * GROUP * use(i, q, SIDES))
                dve.tensor_copy(M[:, g, :, D:ROW].bitcast(I32), Ri[:, :, D:ROW])
                dve.tensor_copy(IX[:, g, :], Ri[:, :, SRC_SLOT])
                dve.wait_ge(a.looked, n + 1)
                dve.tensor_tensor(M[:, g, :, 0:D], PS[:, 2 + g, :].rearrange("p (j f) -> p j f", f=D),
                                  R[:, g, :, 0:D], ALU.mult).then_inc(s_m2, 1)
                regs = blocks_of(DVE, block_of[0], GROUP * n)
                dve.wait_ge(a.summed, n + 1)
                for j in range(GROUP):
                    at = acc_flat[:, bass.ds(regs[j] * D, D)]
                    after_tile_before(a, i, q, j)
                    dve.tensor_tensor(at, PS[:, 4 + g, j * P:(j + 1) * P], at, ALU.add).then_inc(a.added, 1)
            pipeline(dve, (onehots_a, 0), (layer0, 0))

            def onehots_c(i, q):
                d = q % DEEP
                dve.wait_ge(load_c[d], 16 * (use(i, q, DEEP) + 1))
                freed(dve, c.summed, i, q, DEEP)
                for j in range(GROUP):
                    t = dve.tensor_scalar(OHF[:, d, j, :], iota[:, :], S[:, d, j, SRC_IN_BLOCK:SRC_IN_BLOCK + 1].bitcast(I32),
                                          None, ALU.is_equal)
                t.then_inc(c.onehot, 1)
            pipeline(dve, (onehots_c, 0))
            dve.wait_ge(c.summed, GROUPS)

            nroot = [0]

            def norm(to):
                link(dve.tensor_reduce(nsum[:, :], X3, AX_X, ALU.add))
                link(dve.tensor_scalar(nsum[:, :], nsum[:, :], 1.0 / D, None, ALU.mult))
                link(dve.tensor_tensor(X3, X3, nsum[:, :].unsqueeze(2).to_broadcast([P, NB, D]), ALU.subtract))
                link(dve.tensor_tensor(acc[:, :, :], X3, X3, ALU.mult))
                link(dve.tensor_reduce(nsum[:, :], acc[:, :, :], AX_X, ALU.add))
                nroot[0] += 1
                dve.tensor_scalar(nvar[:, :], nsum[:, :], 1.0 / D, EPS, ALU.mult, ALU.add).then_inc(s_var, 1)
                dve.wait_ge(s_std, nroot[0])
                link(dve.reciprocal(rstd[:, :], nvar[:, :]))
                link(dve.tensor_tensor(to, X3, rstd[:, :].unsqueeze(2).to_broadcast([P, NB, D]), ALU.mult))

            def heads(ap):
                return ap.rearrange("p (h f) -> p h f", h=HEADS)

            link(dve.tensor_tensor(X3, X3, acc[:, :, :], ALU.add))
            link(dve.tensor_tensor(X[:, :], X[:, :], SUMS, ALU.add))
            dve.sem_inc(s_tot_c, 1)
            norm(X3)

            dve.wait_ge(s_w, 16 * 8)

            def five(turn, frm, take):
                with dve.Fori(0, NB // 5) as i:
                    n = i + turn * (NB // 5)
                    dve.tensor_copy(stage[:, :, :].rearrange("p b f -> p (b f)"),
                                    frm[:, bass.ds(i * (5 * D), 5 * D)]).then_inc(s_nx, 1)
                    dve.wait_ge(s_nm, n + 1)
                    take(i)

            psum5 = PS[:, 2:4, :].rearrange("p k c -> p (k c)")[:, 0:5 * D]
            Yf = shared[:, 0:o1]

            def take(i):
                dve.tensor_copy(Yf[:, bass.ds(i * (5 * D), 5 * D)], psum5).then_inc(s_nd, 1)
            five(0, X, take)
            dve.wait_ge(s_nd, NB // 5)
            link(dve.tensor_copy(HL[:, :, 0:D], Y[:, :, :]))
            for row, to in ((al_row, HL[:, :, D:D + HEADS]), (ar_row, erm[:, :, 0:HEADS])):
                link(dve.tensor_tensor(acc[:, :, :], Y[:, :, :], row[:, :].unsqueeze(1).to_broadcast([P, NB, D]), ALU.mult))
                link(dve.tensor_reduce(to, acc[:, :, :].rearrange("p b (h f) -> p b h f", h=HEADS), AX_X, ALU.add))

            def three_parts(whole, part):
                n = whole.shape[2]
                spare = rest[:, :, 0:n]
                link(dve.tensor_copy(part(0), whole))
                link(dve.tensor_tensor(spare, whole, part(0), ALU.subtract))
                link(dve.tensor_copy(part(1), spare))
                link(dve.tensor_tensor(spare, spare, part(1), ALU.subtract))
                link(dve.tensor_copy(part(2), spare))

            three_parts(HL[:, :, D:ROW], lambda k: erm_b[:, :, k, 0:HEADS])
            link(dve.tensor_copy(HL[:, :, ROW:WIDE].rearrange("p b (k h) -> p b k h", k=3), erm_b[:, :, :, 0:HEADS]))
            dve.sem_inc(s_tab[0], 1)

            def not_members(i, q):
                g, n = q % SIDES, group(i, q)
                freed(dve, m.summed, i, q, SIDES, GROUP)
                for j in range(GROUP):
                    t = dve.tensor_scalar(NOT[:, g, j, :], iota_b[:, :], dloc[:, bass.ds(GROUP * n + j, 1)],
                                          -1.0, ALU.is_equal, ALU.add)
                t.then_inc(m.onehot, 1)

            def maxima(i, q):
                g, n = q % SIDES, group(i, q)
                regs = blocks_of(DVE, block_of[0], GROUP * n)
                for k in range(2):
                    dve.wait_ge(m.summed, GROUP * n + 2 * k + 2)
                    dve.tensor_reduce(tmax[:, g, 2 * k:2 * k + 2, :],
                                      PS[:, 2 * k:2 * k + 2, :].rearrange("p j (h e) -> p j h e", h=HEADS),
                                      AX_X, ALU.max).then_inc(s_mx, 1)
                dve.wait_ge(s_mx, 2 * n + 2)
                for j in range(GROUP):
                    at = elmax_flat[:, bass.ds(regs[j] * HEADS, HEADS)]
                    after_tile_before(m, i, q, j)
                    dve.tensor_tensor(at, tmax[:, g, j, :], at, ALU.max).then_inc(m.added, 1)
            pipeline(dve, (not_members, 1), (maxima, 0))
            dve.wait_ge(m.added, TILES)
            link(dve.tensor_scalar(elmax[:, :, :], elmax[:, :, :], -1.0e30, None, ALU.max))
            link(dve.tensor_tensor(small[:, :, :], elmax[:, :, :], erm[:, :, 0:HEADS], ALU.add))
            link(dve.tensor_scalar(elmax[:, :, :], small[:, :, :], SLOPE, None, ALU.mult))
            link(dve.tensor_tensor(erm[:, :, HEADS:2 * HEADS], elmax[:, :, :], small[:, :, :], ALU.max))
            three_parts(erm[:, :, :], lambda k: erm_b[:, :, k, :])
            dve.sem_inc(s_tab[0], 1)

            def onehots_w(i, q):
                n, d = group(i, q), q % DEEP
                freed(dve, w.summed, i, q, DEEP)
                for j in range(GROUP):
                    t = dve.tensor_scalar(OHB[:, d, j, :], iota_b[:, :], dloc[:, bass.ds(GROUP * n + j, 1)],
                                          None, ALU.is_equal)
                t.then_inc(w.onehot, 1)

            def logits(i, q):
                g, d, n = q % SIDES, q % DEEP, group(i, q)

                def flat(ap):
                    return ap[:, g, :, :].rearrange("p j h -> p (j h)")
                dve.wait_ge(load_w[d], 16 * (use(i, q, DEEP) + 1))
                dve.wait_ge(s_lc, n + 1)
                dve.tensor_tensor(logit[:, g, :, :], looked[:, d, :, 0:HEADS], S[:, d, :, D:ROW], ALU.add).then_inc(s_lg, 1)
                dve.wait_ge(s_lg, n + 1)
                dve.scalar_tensor_tensor(flat(slope), flat(logit), SLOPE, flat(logit), ALU.mult, ALU.max).then_inc(s_lk, 1)
                dve.wait_ge(s_lk, n + 1)
                dve.tensor_tensor(logit[:, g, :, :], slope[:, g, :, :], looked[:, d, :, HEADS:2 * HEADS],
                                  ALU.subtract).then_inc(s_lg2, 1)
                dve.wait_ge(s_lg2, n + 1)
                freed(dve, s_ex, i, q, SIDES)
                dve.tensor_scalar(shift[:, g, :, :], logit[:, g, :, :], 0.0, None, ALU.min).then_inc(s_sh, 1)

            def messages(i, q):
                d, n = q % DEEP, group(i, q)
                dve.wait_ge(s_ex, n + 1)
                rows = S[:, d, :, 0:D].rearrange("p j (h f) -> p j h f", h=HEADS)
                dve.tensor_tensor(rows, rows, prob[:, d, :, :].unsqueeze(3).to_broadcast([P, GROUP, HEADS, HF]),
                                  ALU.mult).then_inc(w.scaled, 1)

            def take_looked(i, q):
                dve.wait_ge(w.looked, group(i, q) + 1)
                dve.tensor_copy(looked[:, q % DEEP, :, :], LOOKED).then_inc(s_lc, 1)
            pipeline(dve, (onehots_w, 3), (messages, 0), (logits, 1), (take_looked, 2))
            dve.wait_ge(w.summed, GROUPS)
            link(dve.tensor_copy(acc_flat[:, :], SUMS))
            link(dve.tensor_copy(acc1[:, :, :].rearrange("p b f -> p (b f)"), WSUMS))
            dve.sem_inc(s_tot_w, 1)
            for k in (1, 2):
                link(dve.tensor_tensor(acc1[:, :, 0:HEADS], acc1[:, :, 0:HEADS], acc1[:, :, k * HEADS:(k + 1) * HEADS],
                                       ALU.add))
            link(dve.tensor_scalar(small[:, :, :], acc1[:, :, 0:HEADS], 1e-20, None, ALU.max))
            link(dve.reciprocal(elmax[:, :, :], small[:, :, :]))
            for h in range(HEADS):
                at = acc[:, :, h * HF:(h + 1) * HF]
                link(dve.tensor_tensor(acc[:, :, h * HF:(h + 1) * HF], at,
                                       elmax[:, :, h:h + 1].to_broadcast([P, NB, HF]), ALU.mult))
            link(dve.tensor_tensor(acc[:, :, :], acc[:, :, :], X3, ALU.add))
            link(dve.tensor_tensor(acc[:, :, :], acc[:, :, :], b1_row[:, :].unsqueeze(1).to_broadcast([P, NB, D]), ALU.add))
            link(dve.tensor_tensor(X3, X3, acc[:, :, :], ALU.add))
            nroot[0] += 1
            dve.tensor_scalar(dinv[:, :], acc1[:, :, LW - 1], 1.0, None, ALU.add).then_inc(s_var, 1)
            dve.wait_ge(s_std, nroot[0])
            link(dve.reciprocal(dinv[:, :], dinv[:, :]))
            norm(X3)
            dve.sem_inc(s_tab[1], 1)

            def aggregate(p, half):
                def onehots(i, q):
                    n, d = group(i, q), q % DEEP
                    freed(dve, p.summed, i, q, DEEP)
                    for j in range(GROUP):
                        t = dve.tensor_scalar(OHF[:, d, j, :], iota[:, :], dloc[:, bass.ds(GROUP * n + j, 1)],
                                              None, ALU.is_equal)
                    t.then_inc(p.onehot, 1)
                pipeline(dve, (onehots, 0))
                dve.wait_ge(p.summed, GROUPS)
                link(dve.tensor_copy(acc_flat[:, 0:HALF], SUMS[:, 0:HALF]))
                dve.wait_ge(s_half, half)

            aggregate(l2, 1)
            dve.sem_inc(s_tot_2, 1)
            five(1, acc_flat, take)
            dve.wait_ge(s_nd, 2 * (NB // 5))
            link(dve.tensor_tensor(Y[:, :, :], Y[:, :, :], b2_row[:, :].unsqueeze(1).to_broadcast([P, NB, D]), ALU.add))
            link(dve.tensor_tensor(X3, X3, Y[:, :, :], ALU.add))
            norm(X3)
            dve.tensor_tensor(Y[:, :, :], X3, dinv[:, :].unsqueeze(2).to_broadcast([P, NB, D]), ALU.mult).then_inc(s_tab[2], 1)
            dve.wait_ge(s_tab[2], 1)

            aggregate(l3, 2)
            dve.sem_inc(s_tot_3, 1)
            link(dve.tensor_tensor(acc[:, :, :], acc[:, :, :], Y[:, :, :], ALU.add))
            dve.wait_ge(s_tabw[2], 16)
            five(2, acc_flat, take)
            dve.wait_ge(s_nd, 3 * (NB // 5))
            link(dve.tensor_tensor(Y[:, :, :], Y[:, :, :], dinv[:, :].unsqueeze(2).to_broadcast([P, NB, D]), ALU.mult))
            link(dve.tensor_tensor(Y[:, :, :], Y[:, :, :], b3_row[:, :].unsqueeze(1).to_broadcast([P, NB, D]), ALU.add))
            link(dve.tensor_scalar(Y[:, :, :], Y[:, :, :], 0.0, None, ALU.max))
            link(dve.tensor_tensor(X3, X3, Y[:, :, :], ALU.add))
            norm(X3)
            dve.sem_inc(s_fin, 1)


_INS = ['x', 'src', 'dst', 'edge_attr_128', 'L1_gnn_fc_w', 'L1_gnn_attn_l', 'L1_gnn_attn_r', 'L1_gnn_bias',
        'L2_gnn_W', 'L2_gnn_b', 'L3_gnn_W', 'L3_gnn_b']
_OUTS = [((3125, 128), 'float32')]


def kernel(**inputs):
    import numpy as _np
    import concourse.bacc as _bacc
    from concourse import mybir as _mybir
    from concourse.bass_utils import run_bass_kernel_spmd as _run

    nc = _bacc.Bacc("TRN2", target_bir_lowering=False, num_devices=1)
    arrays, args = {}, []
    for name in _INS:
        a = _np.ascontiguousarray(inputs[name])
        arrays[f"in_{name}_dram"] = a
        args.append(nc.dram_tensor(f"in_{name}_dram", a.shape, _mybir.dt.from_np(a.dtype), kind="ExternalInput").ap())
    for i, (shape, dtype) in enumerate(_OUTS):
        dt = _mybir.dt.from_np(_np.dtype(dtype))
        args.append(nc.dram_tensor(f"out_{i}_dram", shape, dt, kind="ExternalOutput").ap())
    gnn_program(nc, *args)
    r = _run(nc, [arrays], core_ids=[0])
    got = tuple(r.results[0][f"out_{i}_dram"] for i in range(len(_OUTS)))
    return got[0]
```

```python
from contextlib import ExitStack

import concourse.bass as bass
from concourse import mybir

ALU = mybir.AluOpType
ACT = mybir.ActivationFunctionType
AX_X = mybir.AxisListType.X
F32 = mybir.dt.float32
BF16 = mybir.dt.bfloat16
I32 = mybir.dt.int32
U32 = mybir.dt.uint32

P = 128
GROUP = 4
SIDES = 2
DEEP = 5
TURN = 10
ROW = 132
SRC, DST, SRC_SLOT, SRC_IN_BLOCK = 128, 129, 130, 131
EPS = 1e-5
FAR = 2.0 ** 100
SLOPE = 0.2
NOWHERE = 255


def gnn_program(nc, x, src, dst, edge_attr, fc_w, attn_l, attn_r, bias1, w2, b2, w3, b3, out):
    N, D = x.shape
    E = src.shape[0]
    HEADS, HF = attn_l.shape
    NB = -(-N // P)
    FULL = N // P
    REST = N - FULL * P
    NP_ = NB * P
    EP = 125
    ET = E // EP
    assert EP * ET == E and D == P and HEADS * HF == D
    NGROUP = 5
    NRING = 5
    NIT = ET // (NGROUP * NRING)
    assert NIT * NGROUP * NRING == ET
    STEP = GROUP * TURN
    TILES = -(-((E + NB * P) // P) // STEP) * STEP
    IT = TILES // STEP
    GROUPS = TILES // GROUP
    SLOTS = TILES * P
    LW = 3 * HEADS + 1
    WIDE = ROW + 3 * HEADS // 2
    BANK = 4
    BANKS = [list(range(b, min(b + BANK, NB))) for b in range(0, NB, BANK)]
    TRIO = 3
    TRIOS = [list(range(b, min(b + TRIO, NB))) for b in range(0, NB, TRIO)]
    HW = D + 2 * HEADS
    ROW2 = D + 1
    ELSEWHERE = 2.0 ** 17
    FULLEST = -(-E // P)
    PADS = TILES - FULLEST
    assert TURN % SIDES == 0 and TURN % DEEP == 0

    meta_d = nc.dram_tensor("meta_d", [E, ROW - D], F32, kind="Internal").ap()
    record = nc.dram_tensor("record", [E, ROW], F32, kind="Internal").ap()
    record2 = nc.dram_tensor("record2", [SLOTS, ROW2], F32, kind="Internal").ap()
    stash = nc.dram_tensor("stash", [TILES, P, ROW], F32, kind="Internal").ap()
    table1 = nc.dram_tensor("table1", [NP_, WIDE], F32, kind="Internal").ap()
    table2 = nc.dram_tensor("table2", [NP_, D], F32, kind="Internal").ap()
    table3 = nc.dram_tensor("table3", [NP_, D], F32, kind="Internal").ap()

    slots2 = record2[0:SLOTS].rearrange("(k p) c -> p k c", p=P)
    stash_v = stash.rearrange("k p c -> p k c")
    edges = edge_attr.rearrange("(p t) f -> p t f", p=EP)

    with ExitStack() as ctx:
        def sb(name, shape, dt=F32):
            return ctx.enter_context(nc.sbuf_tensor(name, shape, dt))

        def sem(name):
            return ctx.enter_context(nc.semaphore(name))

        PS = ctx.enter_context(nc.psum_tensor("PS", [P, 8, 512], F32))

        PSF = PS[:, :, :].rearrange("p k c -> p (k c)")
        SUMS = PSF[:, 0:NB * D]
        WSUMS = PS[:, 6, P:P + NB * LW]
        PARTS = [PS[0:3 * HEADS, 6 + g, :].bitcast(BF16)[:, 0:GROUP * P] for g in range(SIDES)]
        TURNED = PS[:, 7, 0:2 * P].bitcast(BF16)
        LOOKED = PS[:, 7, 2 * P:2 * P + 6 * GROUP * HEADS].rearrange("p (j k) -> p j k", j=GROUP)
        assert NB * D <= 6 * 512 + P and P + NB * LW <= 512

        lane_i = sb("lane_i", [P, 1], I32)
        lane = sb("lane", [P, 1])
        iota_i = sb("iota_i", [P, P], I32)
        iota = sb("iota", [P, P])
        ident = sb("ident", [P, P])
        before = sb("before", [P, P])
        ones = sb("ones", [P, P])
        far_id = sb("far_id", [P, HEADS, P], BF16)
        ones_b = sb("ones_b", [P, P], BF16)
        iota_b = sb("iota_b", [P, P], BF16)
        ident_b = sb("ident_b", [P, P], BF16)
        zeros = sb("zeros", [P, 4 * P], BF16)
        parts_of = sb("parts_of", [3 * HEADS, 3])
        pick = sb("pick", [3 * HEADS, HEADS])
        tile_no_i = sb("tile_no_i", [P, GROUP], I32)
        tile_no = sb("tile_no", [P, GROUP])
        pad = sb("pad", [P, 1, ROW2])
        fcw = sb("fcw", [P, D])
        w2n = sb("w2n", [P, D])
        w2t = sb("w2t", [P, D])
        w3n = sb("w3n", [P, D])
        al_row = sb("al_row", [P, D])
        ar_row = sb("ar_row", [P, D])
        b1_row = sb("b1_row", [P, D])
        b2_row = sb("b2_row", [P, D])
        b3_row = sb("b3_row", [P, D])

        ends = [sb("dst_e", [EP, ET], I32), sb("src_e", [EP, ET], I32)]
        acc = sb("acc", [P, NB, D])
        acc_flat = acc[:, :, :].rearrange("p b f -> p (b f)")

        def setup(n):
            return acc_flat[0:EP, n * ET:(n + 1) * ET]
        blk_i = setup(1).bitcast(I32)
        blk = setup(2)
        end_f = setup(3)
        pos = setup(4)
        shared2 = sb("shared2", [P, NB * ET])
        mask = shared2[0:EP, :].rearrange("p (b t) -> p b t", t=ET)
        shared = sb("shared", [P, NB * ET])
        run = shared[0:EP, :].rearrange("p (b t) -> p b t", t=ET)
        rank = sb("rank", [EP, ET], U32)
        given_i = setup(0).bitcast(I32)
        moved = sb("moved", [EP, 1])
        unsorted = sb("unsorted", [1, 1], I32)
        meta = sb("meta", [EP, ET, 4], I32)
        upto = sb("upto", [EP, NB])
        cnt = sb("cnt", [EP, NB])
        base = sb("base", [EP, NB])
        tot_i = sb("tot_i", [P, NB], I32)
        ntile = sb("ntile", [P, NB])
        last = sb("last", [P, NB])
        first = sb("first", [P, NB])
        past = sb("past", [P, GROUP, NB])
        last_tile = sb("last_tile", [1, NB], I32)
        before_b = sb("before_b", [P, NB])
        short = sb("short", [P, NB])
        lack = sb("lack", [P, GROUP, NB])
        begin = sb("begin", [P, GROUP])
        begin_i = sb("begin_i", [P, GROUP], I32)
        tile_rows = sb("tile_rows", [P, 2, GROUP])
        begin_of = sb("begin_of", [1, TILES], I32)
        rows_of = acc_flat[0:1, 5 * ET:5 * ET + 2 * TILES].rearrange("p (k t) -> p k t", k=2)
        node0 = sb("node0", [P, TILES])
        tblk = sb("tblk", [P, GROUP])
        KINDS = ((HEADS, 0), (P, 0), (LW, 6 * 512 + P), (6 * HEADS, 0))
        MAXIMUM, SUM, WEIGHT, LOGIT = range(4)
        AHEAD = 2
        KINDS_OF = (len(KINDS), 2)
        tblk_i = [sb("tblk_d", [P, KINDS_OF[0], GROUP], I32), sb("tblk_s", [P, KINDS_OF[1], GROUP], I32)]
        columns_of = [sb("columns_of_d", [1, (GROUPS + AHEAD) * GROUP * KINDS_OF[0]], I32),
                      sb("columns_of_s", [1, (GROUPS + AHEAD) * GROUP * KINDS_OF[1]], I32)]

        NR = sb("NR", [EP, NRING, NGROUP, ROW])
        NX = sb("NX", [EP, NRING, NGROUP], U32)
        G = sb("G", [P, DEEP, GROUP, WIDE])
        OHT = sb("OHT", [P, SIDES, GROUP * P])
        NOT = sb("NOT", [P, SIDES, GROUP, P], BF16)
        IX = sb("IX", [P, SIDES, GROUP], U32)
        DL = sb("DL", [P, SIDES, GROUP])
        inside = sb("inside", [P, SIDES, GROUP])
        outside = sb("outside", [P, SIDES, GROUP])
        IX5 = sb("IX5", [P, DEEP, GROUP], U32)
        taken = [0]

        def ring(depth, width):
            lo, hi = taken[0], taken[0] + depth * GROUP * width
            taken[0] = hi
            return shared2[:, lo:hi].rearrange("p (g j f) -> p g j f", g=depth, f=width)
        S = ring(DEEP, ROW)
        OHF = ring(DEEP, P)
        R = ring(SIDES, ROW)
        M = ring(SIDES, ROW2)
        M1 = ring(SIDES, D)
        OH = ring(SIDES, P)
        OHB = sb("OHB", [P, DEEP, GROUP, P], BF16)
        OHTB = sb("OHTB", [P, SIDES, GROUP * P], BF16)
        parts_t = sb("parts_t", [P, SIDES, GROUP, HEADS, P], BF16)
        looked = sb("looked", [P, DEEP, GROUP, 2 * HEADS])
        logit = sb("logit", [P, SIDES, GROUP, HEADS])
        slope = sb("slope", [P, SIDES, GROUP, HEADS])
        shift = sb("shift", [P, SIDES, GROUP, HEADS])
        prob = sb("prob", [P, DEEP, GROUP, HEADS])
        left = sb("left", [P, SIDES, GROUP, HEADS])
        left2 = sb("left2", [P, SIDES, GROUP, HEADS])
        nought = sb("nought", [P, GROUP, HEADS])
        probs = sb("probs", [P, DEEP, GROUP, LW], BF16)
        tmax = sb("tmax", [P, SIDES, GROUP, HEADS])
        src_of = sb("src_of", [P, TILES], U32)
        dloc = sb("dloc", [P, TILES])

        X = sb("X", [P, NB * D])
        X3 = X[:, :].rearrange("p (b f) -> p b f", f=D)
        o1, o3 = NB * D, NB * (D + WIDE)
        Y = shared[:, 0:o1].rearrange("p (b f) -> p b f", f=D)
        HL = shared[:, o1:o3].rearrange("p (b f) -> p b f", f=WIDE)
        Yf = shared[:, 0:o1]
        acc1 = sb("acc1", [P, NB, LW])
        erm = sb("erm", [P, NB, 2 * HEADS])
        erm_b = sb("erm_b", [P, NB, 3, 2 * HEADS], BF16)
        erm_bflat = erm_b[:, :, :, :].rearrange("p b k f -> p (b k f)")
        rest = sb("rest", [P, NB, 2 * HEADS])
        elmax = sb("elmax", [P, NB, HEADS])
        elmax_flat = elmax[:, :, :].rearrange("p b f -> p (b f)")
        xt = sb("xt", [P, 2, TRIO * P])
        fcx = sb("fcx", [P, HW])
        fca = sb("fca", [P, 2, D])
        stats = sb("stats", [P, NB, 6])
        meanvar = sb("meanvar", [P, NB, 2])
        nvar = sb("nvar", [P, NB])
        rstd = sb("rstd", [P, NB])
        dinv = sb("dinv", [P, NB])
        small = sb("small", [P, NB, HEADS])

        s_w = sem("weights_loaded")
        s_x = sem("x_loaded")
        s_ends = sem("ends_loaded")
        s_iota = sem("iotas_made")
        s_dv = sem("vector_chain")
        s_gate = sem("pool_gate")
        s_pad = sem("pad_made")
        s_blank2 = sem("record2_blank")
        s_cnt = sem("counts_made")
        s_tot = sem("counts_summed")
        s_tb = sem("tile_blocks_made")
        s_tbl = sem("tile_blocks_laid")
        s_tr = sem("tile_rows_laid")
        s_node0 = sem("tile_rows_spread")
        s_moved = sem("moved_edges_counted")
        s_movsum = sem("moved_edges_summed")
        s_lt = sem("last_tiles_known")
        s_order = sem("order_known")
        s_metaready = sem("meta_ready")
        s_meta = sem("meta_written")
        s_dl = sem("a_places")
        s_in = sem("a_inside")
        s_clear = sem("x_padding_cleared")
        s_w2 = sem("w2_turned")
        s_nload = [sem(f"edges_loaded{g}") for g in range(NRING)]
        s_nmeta = sem("meta_filled")
        s_nput = [sem(f"edges_put{g}") for g in range(NRING)]

        class Sems:
            def __init__(self, name, stages, load=0, gather=0, put=0):
                def stage(label):
                    return sem(f"{name}_{label}") if label in stages.split() else None
                self.ix = stage("indices")
                self.onehot = stage("onehot")
                self.turned = stage("turned")
                self.onehot_t = stage("onehot_t")
                self.looked = stage("looked_up")
                self.scaled = stage("scaled")
                self.summed = stage("summed")
                self.added = stage("added")
                self.load = [sem(f"{name}_loaded{g}") for g in range(load)]
                self.gather = [sem(f"{name}_gathered{g}") for g in range(gather)]
                self.put = [sem(f"{name}_put{g}") for g in range(put)]

        a = Sems("a", "onehot turned onehot_t looked_up scaled summed added", load=SIDES, gather=DEEP, put=SIDES)
        c = Sems("c", "onehot summed", load=DEEP)
        m = Sems("m", "indices onehot summed added", gather=DEEP, put=DEEP)
        w = Sems("w", "onehot turned onehot_t looked_up scaled summed", load=DEEP)
        l2 = Sems("l2", "indices onehot summed", gather=DEEP)
        l3 = Sems("l3", "indices onehot summed", gather=DEEP)
        s_m2 = sem("a_source_messages")
        s_zero = sem("m_parts_cleared")
        s_mt = sem("m_parts_turned")
        s_mc = sem("m_parts_copied")
        s_mx = sem("m_tile_max")
        s_of = sem("w_onehot_float")
        s_lc = sem("w_looked_up_taken")
        s_pp = [sem(f"w_weight_part{n}") for n in range(5)]
        s_tot_w, s_tot_2 = sem("w_sums_taken"), sem("l2_sums_taken")
        s_c2, s_c3 = sem("l2_sums_copied"), sem("l3_sums_copied")
        s_p2, s_p3 = sem("l2_projected"), sem("l3_projected")
        s_lg = sem("w_logit")
        s_lk = sem("w_leaky")
        s_lg2 = sem("w_less_maximum")
        s_sh = sem("w_shifted")
        s_ex = sem("w_exp")

        s_nx = sem("nodes_ready")
        s_nt = sem("nodes_turned")
        s_ntc = sem("nodes_turned_copied")
        s_nm = sem("nodes_multiplied")
        s_nh = sem("nodes_taken")
        s_ne = sem("node_logits_taken")
        s_var = sem("variance_ready")
        s_std = sem("deviation_ready")
        s_tab = [sem(f"table{n}_ready") for n in range(3)]
        s_tabw = [sem(f"table{n}_written") for n in range(3)]
        s_fin = sem("result_ready")
        s_out = sem("result_written")

        block = ctx.enter_context(nc.Block())

        def again(i):
            return not (isinstance(i, int) and i == 0)

        def turns(eng, n, body):
            body(0)
            with eng.Fori(1, n) as i:
                body(i)

        def pipeline(eng, *stages):
            def at(i, q):
                for body, lead in stages:
                    ii, qq = i + (q + lead) // TURN, (q + lead) % TURN
                    if not isinstance(ii, int) or 0 <= ii < IT:
                        body(ii, qq)
            for q in range(TURN - max(lead for _, lead in stages), TURN):
                at(-1, q)
            for q in range(TURN):
                at(0, q)
            with eng.Fori(1, IT - 1) as i:
                for q in range(TURN):
                    at(i, q)
            for q in range(TURN):
                at(IT - 1, q)

        def group(i, q):
            return TURN * i + q

        def use(i, q, ring):
            return TURN // ring * i + q // ring

        def used(i, q, ring):
            return not isinstance(i, int) or group(i, q) >= ring

        def freed(eng, sem_, i, q, ring, per=1):
            if used(i, q, ring):
                eng.wait_ge(sem_, per * (group(i, q) - ring + 1))

        def columns(eng_type, table, n, kind=SUM, kinds=1):
            why = "the table is clamped to the last block"
            tops = [first_ + (NB - 1) * width for width, first_ in KINDS[kind:kind + kinds]]
            row = GROUP * (len(KINDS) if table is columns_of[0] else KINDS_OF[1])
            at = row * n + (0 if kind == LOGIT else row * AHEAD) + GROUP * kind
            _, regs = nc.values_load_multi_w_load_instructions(
                table[0:1, bass.ds(at, GROUP * kinds)], engines=[eng_type],
                min_val=0, max_val=max(tops), skip_runtime_bounds_check_because=why)
            return [nc.s_assert_within(reg, 0, tops[k // GROUP], skip_runtime_bounds_check_because=why) for k, reg in enumerate(regs)]

        def order_unknown(eng_type):
            _, regs = nc.values_load_multi_w_load_instructions(
                unsorted[0:1, 0:1], engines=[eng_type], min_val=0, max_val=1,
                skip_runtime_bounds_check_because="the flag is clamped to one")
            return regs[0]

        @block.sync
        def _(sp):
            for e, given in zip(ends, (dst, src)):
                sp.dma_start(e[:, :], given.rearrange("(p t) -> p t", p=EP)).then_inc(s_ends, 16)
            sp.dma_start(X3[:, 0:FULL, :], x[0:FULL * P, :].rearrange("(b p) f -> p b f", p=P)).then_inc(s_x, 16)
            sp.wait_ge(s_clear, 1)
            sp.dma_start(X3[0:REST, FULL, :], x[FULL * P:N, :]).then_inc(s_x, 16)
            for t, given in ((fcw, fc_w), (w2n, w2), (w3n, w3)):
                sp.dma_start(t[:, :], given).then_inc(s_w, 16)
            for t, given in ((al_row, attn_l.rearrange("h f -> (h f)")), (ar_row, attn_r.rearrange("h f -> (h f)")),
                             (b1_row, bias1), (b2_row, b2), (b3_row, b3)):
                sp.dma_start(t[:, :], given.partition_broadcast(P)).then_inc(s_w, 16)
            def in_a_row(ap, q=GROUP):
                return ap.rearrange("a (p q) -> a p q", q=q)
            for n in range(2):
                sp.wait_ge(s_tb, n + 1)
                row = in_a_row(columns_of[n][0:1, :], KINDS_OF[n] * GROUP)
                kinds = tblk_i[n][0:GROUPS, :, :].rearrange("p k q -> p (k q)")
                near = GROUP * min(LOGIT, KINDS_OF[n])
                sp.dma_start(row[:, AHEAD:AHEAD + GROUPS, 0:near], kinds[:, 0:near]).then_inc(s_tbl, 16)
                if n == 0:
                    sp.dma_start(row[:, 0:GROUPS, near:near + GROUP], kinds[:, near:near + GROUP]).then_inc(s_tbl, 16)
                if n == 0:
                    sp.dma_start(in_a_row(begin_of[0:1, :]), begin_i[0:GROUPS, :]).then_inc(s_tbl, 16)
                    for k in range(2):
                        sp.dma_start(in_a_row(rows_of[0:1, k, :]), tile_rows[0:GROUPS, k, :]).then_inc(s_tr, 16)

            def load_edges(i):
                for g in range(NRING):
                    if again(i):
                        sp.wait_ge(s_nput[g], 16 * NGROUP * i)
                    sp.dma_start(NR[:, g, :, 0:D],
                                 edges[:, bass.ds((i * NRING + g) * NGROUP, NGROUP), :]).then_inc(s_nload[g], 16)

            def tiles(i, q):
                return bass.ds(GROUP * group(i, q), GROUP)

            SP = mybir.EngineType.SP

            def load_records(features, integers):
                def step(i, q):
                    g = q % SIDES
                    _, rows = nc.values_load_multi_w_load_instructions(
                        begin_of[0:1, bass.ds(GROUP * group(i, q), GROUP)], engines=[SP], min_val=0, max_val=E - P,
                        skip_runtime_bounds_check_because="the table is clamped to the last edges")
                    freed(sp, s_m2, i, q, SIDES)
                    for j in range(GROUP):
                        at = bass.ds(rows[j], P)
                        sp.dma_start(R[:, g, j, 0:D], features[at, :]).then_inc(a.load[g], 16)
                        sp.dma_start(R[:, g, j, D:ROW], integers[at, :]).then_inc(a.load[g], 16)
                pipeline(sp, (step, 0))

            sp.wait_ge(s_tbl, 64)
            sp.wait_ge(s_order, 1)
            with sp.If(order_unknown(SP)):
                turns(sp, NIT, load_edges)
                for g in range(NRING):
                    sp.wait_ge(s_nput[g], 16 * NGROUP * NIT)
                load_records(record[:, 0:D], record[:, D:ROW])
            with sp.Else():
                sp.wait_ge(s_metaready, 1)
                sp.dma_start(meta_d.rearrange("(p t) c -> p t c", p=EP).bitcast(I32), meta[:, :, :]).then_inc(s_meta, 16)
                sp.wait_ge(s_meta, 16)
                load_records(edge_attr, meta_d)

            for g in range(SIDES):
                sp.wait_ge(a.put[g], 16 * TILES // SIDES)

            def load_records2(i, q):
                freed(sp, c.summed, i, q, DEEP)
                sp.dma_start(S[:, q % DEEP, :, 0:ROW2], slots2[:, tiles(i, q), :]).then_inc(c.load[q % DEEP], 16)
            pipeline(sp, (load_records2, 0))

            sp.wait_ge(s_tab[0], 1)
            sp.dma_start(table1.rearrange("(b p) c -> p b c", p=P), HL[:, :, :]).then_inc(s_tabw[0], 16)

            def keep_rows(i, q):
                d = q % DEEP
                sp.wait_ge(m.gather[d], 16 * GROUP * (use(i, q, DEEP) + 1))
                sp.dma_start(stash_v[:, tiles(i, q), :], G[:, d, :, 0:ROW]).then_inc(m.put[d], 16)
            pipeline(sp, (keep_rows, 0))
            for d in range(DEEP):
                sp.wait_ge(m.put[d], 16 * GROUPS // DEEP)

            def load_rows(i, q):
                freed(sp, w.summed, i, q, DEEP)
                sp.dma_start(S[:, q % DEEP, :, :], stash_v[:, tiles(i, q), :]).then_inc(w.load[q % DEEP], 16)
            pipeline(sp, (load_rows, 0))

            sp.wait_ge(s_tab[1], 1)
            sp.dma_start(table2.rearrange("(b p) c -> p b c", p=P), X3).then_inc(s_tabw[1], 16)
            sp.wait_ge(s_tab[2], 1)
            sp.dma_start(table3.rearrange("(b p) c -> p b c", p=P), Y[:, :, :]).then_inc(s_tabw[2], 16)
            sp.wait_ge(s_fin, 1)
            sp.dma_start(out[0:FULL * P, :].rearrange("(b p) f -> p b f", p=P), X3[:, 0:FULL, :]).then_inc(s_out, 16)
            sp.dma_start(out[FULL * P:N, :], X3[0:REST, FULL, :]).then_inc(s_out, 16)
            sp.wait_ge(s_out, 32)
            sp.wait_ge(s_blank2, 16 * (NB + 1))
            for n in range(3):
                sp.wait_ge(s_tabw[n], 16)

        @block.gpsimd
        def _(pool):
            def row_index(ap):
                return bass.IndirectOffsetOnAxis(ap, 0)

            pool.iota(iota_i[:, :], [[1, P]], base=0, channel_multiplier=0).then_inc(s_iota, 1)
            pool.iota(lane_i[:, :], [[0, 1]], base=0, channel_multiplier=1).then_inc(s_iota, 1)
            pool.iota(tile_no_i[:, :], [[1, GROUP]], base=0, channel_multiplier=GROUP).then_inc(s_iota, 1)
            pool.iota(given_i[:, :], [[1, ET]], base=0, channel_multiplier=ET).then_inc(s_iota, 1)
            pool.memset(pad[:, :, :], 0.0).then_inc(s_iota, 1)
            pool.memset(parts_t[:, :, :, :, :], 0.0).then_inc(s_zero, 1)


            def put_edges(i):
                for g in range(NRING):
                    pool.wait_ge(s_nload[g], 16 * (i + 1))
                    pool.wait_ge(s_nmeta, NRING * i + g + 1)
                    pool.sem_inc(s_gate, 1)
                    for j in range(NGROUP):
                        pool.indirect_dma_start(record[:, :], row_index(NX[:, g, j:j + 1]), NR[:, g, j, :],
                                                None).then_inc(s_nput[g], 16)
            pool.wait_ge(s_order, 1)
            with pool.If(order_unknown(mybir.EngineType.Pool)):
                turns(pool, NIT, put_edges)
            pool.wait_ge(s_blank2, 16 * (NB + 1))

            def gather_x(i, q):
                g, d = q % SIDES, q % DEEP
                pool.wait_ge(a.load[g], 32 * GROUP * (use(i, q, SIDES) + 1))
                freed(pool, a.scaled, i, q, DEEP)
                pool.sem_inc(s_gate, 1)
                for j in range(GROUP):
                    pool.indirect_dma_start(G[:, d, j, 0:D], None, x[:, :],
                                            row_index(R[:, g, j, SRC:SRC + 1].bitcast(U32))).then_inc(a.gather[d], 16)

            def put_messages(i, q):
                g = q % SIDES
                pool.wait_ge(s_m2, group(i, q) + 1)
                pool.sem_inc(s_gate, 1)
                for j in range(GROUP):
                    pool.indirect_dma_start(record2[:, :], row_index(IX[:, g, j:j + 1]),
                                            M[:, g, j, :], None, bounds_check=SLOTS - 1,
                                            oob_is_err=False).then_inc(a.put[g], 16)
            pipeline(pool, (gather_x, 1), (put_messages, 0))

            def gather_rows(p, table, width, free, per=1):
                def step(i, q):
                    d = q % DEEP
                    pool.wait_ge(p.ix, group(i, q) + 1)
                    freed(pool, free, i, q, DEEP, per)
                    if p is m and used(i, q, DEEP):
                        pool.wait_ge(m.put[d], 16 * use(i, q, DEEP))
                    pool.sem_inc(s_gate, 1)
                    for j in range(GROUP):
                        pool.indirect_dma_start(G[:, d, j, 0:width], None, table[:, :],
                                                row_index(IX5[:, d, j:j + 1])).then_inc(p.gather[d], 16)
                pipeline(pool, (step, 0))

            pool.wait_ge(s_tabw[0], 16)
            gather_rows(m, table1, WIDE, m.summed, GROUP)

            def split(i, q):
                g, d = q % SIDES, q % DEEP
                n = group(i, q) + 1
                pool.wait_ge(s_ex, n)
                freed(pool, w.summed, i, q, DEEP)
                pool.sem_inc(s_gate, 1)
                pool.tensor_tensor(probs[:, d, :, 0:HEADS], prob[:, d, :, :], nought[:, :, :], ALU.add).then_inc(s_pp[0], 1)
                pool.wait_ge(s_pp[0], n)
                pool.tensor_tensor(left[:, g, :, :], prob[:, d, :, :], probs[:, d, :, 0:HEADS], ALU.subtract).then_inc(s_pp[1], 1)
                pool.wait_ge(s_pp[1], n)
                pool.tensor_tensor(probs[:, d, :, HEADS:2 * HEADS], left[:, g, :, :], nought[:, :, :], ALU.add).then_inc(s_pp[2], 1)
                pool.wait_ge(s_pp[2], n)
                pool.tensor_tensor(left2[:, g, :, :], left[:, g, :, :], probs[:, d, :, HEADS:2 * HEADS], ALU.subtract).then_inc(s_pp[3], 1)
                pool.wait_ge(s_pp[3], n)
                pool.tensor_tensor(probs[:, d, :, 2 * HEADS:3 * HEADS], left2[:, g, :, :], nought[:, :, :], ALU.add).then_inc(s_pp[4], 1)
            pipeline(pool, (split, 0))

            for d in range(DEEP):
                pool.wait_ge(m.put[d], 16 * GROUPS // DEEP)
            pool.wait_ge(s_tabw[1], 16)
            gather_rows(l2, table2, D, l2.summed)
            pool.wait_ge(s_tabw[2], 16)
            gather_rows(l3, table3, D, l3.summed)

        @block.tensor
        def _(pe):
            for n in range(2):
                pe.wait_ge(s_cnt, n + 1)
                pe.matmul(PS[0:EP, 0, 0:NB], before[0:EP, 0:EP], cnt[:, :], start=True, stop=True)
                pe.matmul(PS[:, 1, 0:NB], ones[0:EP, :], cnt[:, :], start=True, stop=True).then_inc(s_tot, 1)
            pe.wait_ge(s_tr, 32)
            for k in range(2):
                t = pe.matmul(PS[:, 2 + k, 0:TILES], ones[0:1, :], rows_of[0:1, k, :], start=True, stop=True)
            t.then_inc(s_node0, 1)
            pe.wait_ge(s_moved, 1)
            pe.matmul(PS[:, 4, 0:1], ones[0:EP, :], moved[:, :], start=True, stop=True).then_inc(s_movsum, 1)
            pe.wait_ge(s_w, 16 * 8)
            pe.transpose(PS[:, 7, 0:P], w2n[:, :], ident[:, :]).then_inc(s_w2, 1)

            PE = mybir.EngineType.PE

            pe.wait_ge(s_tbl, 64)
            pe.wait_ge(s_x, 32)

            def look_up(i, q):
                g, n = q % SIDES, group(i, q)
                pe.wait_ge(a.onehot, n + 1)
                freed(pe, a.onehot_t, i, q, SIDES)
                for j in range(GROUP):
                    t = pe.transpose(PS[:, g, j * P:(j + 1) * P], OH[:, g, j, :], ident[:, :])
                t.then_inc(a.turned, 1)
                regs = columns(PE, columns_of[0], n)
                pe.wait_ge(a.onehot_t, n + 1)
                freed(pe, s_m2, i, q, SIDES)
                for j in range(GROUP):
                    t = pe.matmul(PS[:, 2 + g, j * P:(j + 1) * P], OHT[:, g, j * P:(j + 1) * P],
                                  X[:, bass.ds(regs[j], D)], start=True, stop=True)
                t.then_inc(a.looked, 1)

            def sum_a(i, q):
                g, n = q % SIDES, group(i, q)
                pe.wait_ge(a.scaled, n + 1)
                freed(pe, a.added, i, q, SIDES, GROUP)
                for j in range(GROUP):
                    t = pe.matmul(PS[:, 4 + g, j * P:(j + 1) * P], OH[:, g, j, :], M1[:, g, j, :], start=True, stop=True)
                t.then_inc(a.summed, 1)
            pipeline(pe, (look_up, 0), (sum_a, 0))

            def clear_sums():
                for b in range(7):
                    t = pe.matmul(PS[:, b, :], zeros[:, 0:P], zeros[:, :], start=True, stop=True)

            def sum_into_blocks(p, table, rows, arrived, per, features_down):
                def step(i, q):
                    d, n = q % DEEP, group(i, q)
                    regs = columns(PE, table, n)
                    pe.wait_ge(p.onehot, n + 1)
                    pe.wait_ge(arrived[d], per * (use(i, q, DEEP) + 1))
                    for j in range(GROUP):
                        onehot, row = OHF[:, d, j, :], rows[:, d, j, 0:D]
                        left_, right = (row, onehot) if features_down else (onehot, row)
                        t = pe.matmul(SUMS[:, bass.ds(regs[j], D)], left_, right,
                                      start=False, stop=True, skip_group_check=True)
                    t.then_inc(p.summed, 1)
                pipeline(pe, (step, 0))

            pe.wait_ge(a.added, TILES)
            clear_sums()
            sum_into_blocks(c, columns_of[1], S, c.load, 16, False)

            pe.wait_ge(s_nx, 1)

            def turn_nodes(t):
                if t >= 2:
                    pe.wait_ge(s_ntc, t - 1)
                for n, b in enumerate(TRIOS[t]):
                    last = pe.transpose(PS[:, t % 2, n * P:(n + 1) * P], X3[:, b, :], ident[:, :])
                last.then_inc(s_nt, 1)
            turn_nodes(0)
            for t in range(len(TRIOS)):
                if t + 1 < len(TRIOS):
                    turn_nodes(t + 1)
                pe.wait_ge(s_ntc, t + 1)
                if t >= 2:
                    pe.wait_ge(s_nh, t - 1)
                    pe.wait_ge(s_ne, t - 1)
                for n, b in enumerate(TRIOS[t]):
                    last = pe.matmul(PS[:, 2 + t % 2, n * HW:(n + 1) * HW], xt[:, t % 2, n * P:(n + 1) * P], fcx[:, :],
                                     start=True, stop=True)
                last.then_inc(s_nm, 1)
            pe.wait_ge(s_nh, len(TRIOS))
            pe.wait_ge(s_ne, len(TRIOS))

            def project(weights, taken, done):
                for k, blocks in enumerate(BANKS):
                    pe.wait_ge(taken, k + 1)
                    for b in blocks:
                        last = pe.matmul(SUMS[:, b * D:(b + 1) * D], acc_flat[:, b * D:(b + 1) * D], weights[:, :],
                                         start=True, stop=True)
                    last.then_inc(done, 1)

            def turn_parts(i, q):
                g, d, n = q % SIDES, q % DEEP, group(i, q)
                pe.wait_ge(m.gather[d], 16 * GROUP * (use(i, q, DEEP) + 1))
                freed(pe, s_mc, i, q, SIDES)
                for j in range(GROUP):
                    t = pe.transpose(PARTS[g][:, j * P:(j + 1) * P], G[:, d, j, ROW:WIDE].bitcast(BF16), ident_b[:, :])
                t.then_inc(s_mt, 1)

            def maxima(i, q):
                g, n = q % SIDES, group(i, q)
                pe.wait_ge(m.onehot, n + 1)
                pe.wait_ge(s_mc, n + 1)
                for j in range(GROUP):
                    if j % 2 == 0 and used(i, q, 1):
                        pe.wait_ge(s_mx, 2 * n - 1 + j // 2)
                    pe.matmul(PS[:, j, :], NOT[:, g, j, :], far_id[:, :, :].rearrange("p h e -> p (h e)"),
                              start=True, stop=False)
                    pe.matmul(PS[:, j, :], ones_b[:, :], parts_t[:, g, j, :, :].rearrange("p h e -> p (h e)"),
                              start=False, stop=True).then_inc(m.summed, 1)
            pipeline(pe, (turn_parts, 1), (maxima, 0))

            pe.wait_ge(s_tab[0], 2)
            clear_sums()

            held = []

            def turn_onehot(i, q):
                pe.wait_ge(w.onehot, group(i, q) + 1)
                freed(pe, s_lc, i, q, 1)
                for j in range(GROUP):
                    t = pe.transpose(TURNED[:, j * P:(j + 1) * P], OHB[:, q % DEEP, j, :], ident_b[:, :])
                t.then_inc(w.turned, 1)

            def look_up_logits(i, q):
                g, n = q % SIDES, group(i, q)
                regs = columns(PE, columns_of[0], n, LOGIT) if isinstance(n, int) and n < AHEAD else held[2 * GROUP:]
                pe.wait_ge(w.onehot_t, n + 1)
                for j in range(GROUP):
                    t = pe.matmul(LOOKED[:, j, :], OHTB[:, g, j * P:(j + 1) * P],
                                  erm_bflat[:, bass.ds(regs[j], 6 * HEADS)], start=True, stop=True)
                t.then_inc(w.looked, 1)

            def load_columns(i, q):
                n = group(i, q)
                held[:] = columns(PE, columns_of[0], n, SUM, 2 if isinstance(n, int) and n + AHEAD >= GROUPS else 3)

            def sum_rows(tiles, i, q):
                for j in tiles:
                    pe.matmul(PSF[:, bass.ds(held[j], D)], OHF[:, q % DEEP, j, :], S[:, q % DEEP, j, 0:D],
                              start=False, stop=True, skip_group_check=True)

            def sum_first_half(i, q):
                n = group(i, q)
                pe.wait_ge(s_of, n + 1)
                pe.wait_ge(w.scaled, n + 1)
                sum_rows(range(GROUP // 2), i, q)

            def sum_second_half(i, q):
                d, n = q % DEEP, group(i, q)
                sum_rows(range(GROUP // 2, GROUP), i, q)
                pe.wait_ge(s_pp[4], n + 1)
                for j in range(GROUP):
                    t = pe.matmul(PSF[:, bass.ds(held[GROUP + j], LW)], OHB[:, d, j, :], probs[:, d, j, :],
                                  start=False, stop=True, skip_group_check=True)
                t.then_inc(w.summed, 1)
            pipeline(pe, (load_columns, 0), (look_up_logits, AHEAD), (sum_first_half, 0), (turn_onehot, 3), (sum_second_half, 0))

            pe.wait_ge(s_tot_w, 1)
            clear_sums()
            sum_into_blocks(l2, columns_of[0], G, l2.gather, 16 * GROUP, True)
            project(w2t, s_c2, s_p2)

            pe.wait_ge(s_tot_2, 1)
            clear_sums()
            for b in range(NB):
                pe.matmul(SUMS[:, b * D:(b + 1) * D], Y[:, b, :], ident[:, :], start=False, stop=True,
                          skip_group_check=True)
            sum_into_blocks(l3, columns_of[0], G, l3.gather, 16 * GROUP, True)
            project(w3n, s_c3, s_p3)

        @block.scalar
        def _(act):
            act.wait_ge(s_pad, 1)
            act.wait_ge(s_lt, 1)
            with act.Fori(0, NB) as b:
                _, tile = nc.values_load_multi_w_load_instructions(
                    last_tile[0:1, bass.ds(b, 1)], engines=[mybir.EngineType.Activation], min_val=0, max_val=TILES - 1,
                    skip_runtime_bounds_check_because="all blocks together have no more than TILES tiles")
                act.dma_start(slots2[:, bass.ds(tile[0], 1), :], pad[:, :, :]).then_inc(s_blank2, 16)
            act.wait_ge(s_blank2, 16 * NB)
            act.dma_start(slots2[:, FULLEST:TILES, :], pad[:, :, :].to_broadcast([P, PADS, ROW2])).then_inc(s_blank2, 16)

            def copy_turned(i, q):
                g, n = q % SIDES, group(i, q)
                act.wait_ge(a.turned, n + 1)
                freed(act, a.looked, i, q, SIDES)
                act.activation(OHT[:, g, :], PS[:, g, :], ACT.Copy).then_inc(a.onehot_t, 1)

            def root(n):
                act.wait_ge(s_var, n)
                act.activation(nvar[:, :], nvar[:, :], ACT.Sqrt).then_inc(s_std, 1)

            pipeline(act, (copy_turned, 0))
            root(1)

            for t, blocks in enumerate(TRIOS):
                n, b = len(blocks), blocks[0]
                act.wait_ge(s_nt, t + 1)
                if t >= 2:
                    act.wait_ge(s_nm, t - 1)
                act.activation(xt[:, t % 2, 0:n * P], PS[:, t % 2, 0:n * P], ACT.Copy).then_inc(s_ntc, 1)
                act.wait_ge(s_nm, t + 1)
                act.activation(HL[:, b:b + n, 0:ROW], PS[:, 2 + t % 2, 0:n * HW].rearrange("p (b c) -> p b c", c=HW)[:, :, 0:ROW],
                               ACT.Copy).then_inc(s_nh, 1)

            act.wait_ge(s_zero, 1)

            def indices_of(p):
                def step(i, q):
                    d = q % DEEP
                    if used(i, q, DEEP):
                        act.wait_ge(p.gather[d], 16 * GROUP * use(i, q, DEEP))
                    act.activation(IX5[:, d, :], src_of[:, bass.ds(GROUP * group(i, q), GROUP)], ACT.Copy).then_inc(p.ix, 1)
                return step

            def copy_parts(i, q):
                g, n = q % SIDES, group(i, q)
                act.wait_ge(s_mt, n + 1)
                freed(act, m.summed, i, q, SIDES, GROUP)
                for h in range(HEADS):
                    t = act.activation(parts_t[0:3 * HEADS, g, :, h, :], PARTS[g].rearrange("p (j e) -> p j e", e=P), ACT.Copy,
                                       scale=pick[:, h:h + 1])
                t.then_inc(s_mc, 1)
            pipeline(act, (indices_of(m), 4), (copy_parts, 0))

            def copy_onehots(i, q):
                g, d, n = q % SIDES, q % DEEP, group(i, q)
                act.wait_ge(w.turned, n + 1)
                freed(act, w.looked, i, q, SIDES)
                act.activation(OHTB[:, g, :], TURNED, ACT.Copy).then_inc(w.onehot_t, 1)
                freed(act, w.summed, i, q, DEEP)
                act.activation(OHF[:, d, :, :], OHB[:, d, :, :], ACT.Copy).then_inc(s_of, 1)

            def weights(i, q):
                act.wait_ge(s_sh, group(i, q) + 1)
                freed(act, w.summed, i, q, DEEP)
                act.activation(prob[:, q % DEEP, :, :], shift[:, q % SIDES, :, :], ACT.Exp).then_inc(s_ex, 1)
            pipeline(act, (weights, 1), (copy_onehots, 3))
            act.wait_ge(s_var, 2)
            act.activation(dinv[:, :], dinv[:, :], ACT.Sqrt).then_inc(s_std, 1)
            root(3)

            def copy_sums(p, copied):
                pipeline(act, (indices_of(p), 0))
                act.wait_ge(p.summed, GROUPS)
                for blocks in BANKS:
                    lo, hi = blocks[0] * D, (blocks[-1] + 1) * D
                    act.activation(acc_flat[:, lo:hi], SUMS[:, lo:hi], ACT.Copy).then_inc(copied, 1)
            copy_sums(l2, s_c2)
            root(4)
            copy_sums(l3, s_c3)
            root(5)

        @block.vector
        def _(dve):
            done = [0]

            def link(ins):
                done[0] += 1
                ins.then_inc(s_dv, 1)
                dve.wait_ge(s_dv, done[0])

            dve.memset(X3[:, FULL, :], 0.0).then_inc(s_clear, 1)
            dve.wait_ge(s_iota, 5)
            link(dve.tensor_copy(iota[:, :], iota_i[:, :]))
            link(dve.tensor_copy(lane[:, :], lane_i[:, :]))
            link(dve.tensor_copy(tile_no[:, :], tile_no_i[:, :]))
            link(dve.tensor_scalar(ident[:, :], iota[:, :], lane[:, 0:1], None, ALU.is_equal))
            dve.tensor_scalar(before[:, :], iota[:, :], lane[:, 0:1], None, ALU.is_gt)
            dve.memset(ones[:, :], 1.0)
            dve.tensor_copy(iota_b[:, :], iota_i[:, :])
            dve.tensor_copy(ident_b[:, :], ident[:, :])
            dve.memset(zeros[:, :], 0.0)
            dve.memset(nought[:, :, :], 0.0)
            dve.memset(probs[:, :, :, LW - 1:LW], 1.0)
            link(dve.tensor_scalar(parts_of[:, 0:1], lane[0:3 * HEADS, :], float(HEADS), None, ALU.is_ge))
            link(dve.tensor_scalar(parts_of[:, 1:2], lane[0:3 * HEADS, :], float(2 * HEADS), None, ALU.is_ge))
            link(dve.tensor_tensor(parts_of[:, 0:1], parts_of[:, 0:1], parts_of[:, 1:2], ALU.add))
            link(dve.scalar_tensor_tensor(parts_of[:, 2:3], parts_of[:, 0:1], -float(HEADS), lane[0:3 * HEADS, :],
                                          ALU.mult, ALU.add))
            for h in range(HEADS):
                dve.tensor_scalar(pick[:, h:h + 1], parts_of[:, 2:3], float(h), None, ALU.is_equal)
            dve.memset(ones_b[:, :], 1.0)
            for h in range(HEADS):
                dve.tensor_scalar(far_id[:, h, :], ident[:, :], FAR, None, ALU.mult)
            pad_int = pad[:, :, :].bitcast(I32)
            dve.tensor_scalar(pad_int[:, :, D], pad_int[:, :, 0], float(NOWHERE), None, ALU.add).then_inc(s_pad, 1)

            dve.wait_ge(s_ends, 32)
            for n in range(2):
                link(dve.tensor_copy(end_f[:, :], ends[n][:, :]))
                link(dve.tensor_scalar(blk_i[:, :], ends[n][:, :], 7, None, ALU.arith_shift_right))
                link(dve.tensor_copy(blk[:, :], blk_i[:, :]))
                if n == 0:
                    link(dve.tensor_copy(meta[:, :, DST - D], ends[0][:, :]))
                else:
                    link(dve.scalar_tensor_tensor(meta[:, :, SRC_IN_BLOCK - D], blk[:, :], -float(P), end_f[:, :],
                                                  ALU.mult, ALU.add))
                    link(dve.tensor_copy(meta[:, :, SRC - D], ends[1][:, :]))
                link(dve.tensor_tensor(mask[:, :, :], blk[:, :].unsqueeze(1).to_broadcast([EP, NB, ET]),
                                       iota[0:EP, 0:NB].unsqueeze(2).to_broadcast([EP, NB, ET]), ALU.is_equal))
                flat_run = shared[0:EP, :]
                flat_mask = shared2[0:EP, :]
                link(dve.tensor_tensor_scan(flat_run, flat_mask, flat_mask, 0.0, ALU.add, ALU.max))
                link(dve.tensor_copy(upto[:, :], run[:, :, ET - 1]))
                link(dve.tensor_copy(cnt[:, 0:1], upto[:, 0:1]))
                dve.tensor_tensor(cnt[:, 1:NB], upto[:, 1:NB], upto[:, 0:NB - 1], ALU.subtract).then_inc(s_cnt, 1)
                dve.wait_ge(s_tot, n + 1)
                link(dve.tensor_scalar(tot_i[:, :], PS[:, 1, 0:NB], float(P - 1), None, ALU.add))
                link(dve.tensor_scalar(tot_i[:, :], tot_i[:, :], 7, None, ALU.arith_shift_right))
                link(dve.tensor_scalar(ntile[:, :], tot_i[:, :], 1.0, None, ALU.max))
                link(dve.tensor_tensor_scan(last[:, :], ntile[:, :], ntile[:, :], 0.0, ALU.add, ALU.max))
                link(dve.tensor_tensor(first[:, :], last[:, :], ntile[:, :], ALU.subtract))
                if n == 1:
                    dve.tensor_scalar(last_tile[:, :], last[0:1, :], -1.0, None, ALU.add).then_inc(s_lt, 1)
                if n == 0:
                    link(dve.tensor_scalar(short[:, :], PS[:, 1, 0:NB], 0.0, None, ALU.add))
                    link(dve.tensor_tensor_scan(before_b[:, :], short[:, :], short[:, :], 0.0, ALU.add, ALU.max))
                    link(dve.tensor_tensor(before_b[:, :], before_b[:, :], short[:, :], ALU.subtract))
                    link(dve.scalar_tensor_tensor(short[:, :], ntile[:, :], -float(P), short[:, :], ALU.mult, ALU.add))
                    link(dve.tensor_tensor(base[:, :], before_b[0:EP, :], PS[0:EP, 0, 0:NB], ALU.add))
                else:
                    link(dve.scalar_tensor_tensor(base[:, :], first[0:EP, :], float(P), PS[0:EP, 0, 0:NB],
                                                  ALU.mult, ALU.add))
                link(dve.tensor_tensor(base[:, :], base[:, :], upto[:, :], ALU.subtract))
                link(dve.tensor_tensor(base[:, :], base[:, :], cnt[:, :], ALU.add))
                link(dve.tensor_scalar(base[:, :], base[:, :], -1.0, None, ALU.add))
                for b in range(NB):
                    end = dve.scalar_tensor_tensor(run[:, b, :], run[:, b, :], base[:, b:b + 1], mask[:, b, :],
                                                   ALU.add, ALU.mult)
                link(end)
                link(dve.tensor_reduce(pos[:, :], run[:, :, :].rearrange("p b t -> p t b"), AX_X, ALU.add))
                if n == 0:
                    link(dve.tensor_copy(rank[:, :], pos[:, :]))
                    link(dve.tensor_copy(end_f[:, :], given_i[:, :]))
                    link(dve.tensor_tensor(end_f[:, :], end_f[:, :], pos[:, :], ALU.not_equal))
                    dve.tensor_reduce(moved[:, :], end_f[:, :], AX_X, ALU.add).then_inc(s_moved, 1)
                else:
                    link(dve.tensor_scalar(pos[:, :], pos[:, :], float(SLOTS), None, ALU.add))
                    dve.tensor_copy(meta[:, :, SRC_SLOT - D], pos[:, :]).then_inc(s_metaready, 1)
                link(dve.tensor_tensor(past[:, :, :], tile_no[:, :].unsqueeze(2).to_broadcast([P, GROUP, NB]),
                                       last[:, :].unsqueeze(1).to_broadcast([P, GROUP, NB]), ALU.is_ge))
                link(dve.tensor_reduce(tblk[:, :], past[:, :, :], AX_X, ALU.add))
                if n == 0:
                    link(dve.tensor_tensor(lack[:, :, :], past[:, :, :],
                                           short[:, :].unsqueeze(1).to_broadcast([P, GROUP, NB]), ALU.mult))
                    link(dve.tensor_reduce(begin[:, :], lack[:, :, :], AX_X, ALU.add))
                    link(dve.scalar_tensor_tensor(begin[:, :], tile_no[:, :], float(P), begin[:, :], ALU.mult, ALU.add))
                    link(dve.tensor_scalar(begin_i[:, :], begin[:, :], float(E - P), None, ALU.min))
                    link(dve.tensor_scalar(tile_rows[:, 1, :], begin[:, :], -float(E - P), 0.0, ALU.add, ALU.max))
                    link(dve.tensor_scalar(tile_rows[:, 0, :], tblk[:, :], float(NB - 1), float(P), ALU.min, ALU.mult))
                link(dve.tensor_scalar(tblk[:, :], tblk[:, :], float(NB - 1), None, ALU.min))
                for kind, (width, first_) in enumerate(KINDS[:KINDS_OF[n]]):
                    end = dve.tensor_scalar(tblk_i[n][:, kind, :], tblk[:, :], float(width), float(first_),
                                            ALU.mult, ALU.add)
                end.then_inc(s_tb, 1)
            dve.wait_ge(s_movsum, 1)
            dve.tensor_scalar(unsorted[:, :], PS[0:1, 4, 0:1], 1.0, None, ALU.min).then_inc(s_order, 1)
            dve.wait_ge(s_node0, 1)
            link(dve.tensor_scalar(node0[:, :], PS[:, 3, 0:TILES], lane[:, 0:1], ELSEWHERE, ALU.is_gt, ALU.mult))
            link(dve.tensor_tensor(node0[:, :], node0[:, :], PS[:, 2, 0:TILES], ALU.add))

            def fill_meta(i):
                for g in range(NRING):
                    if again(i):
                        dve.wait_ge(s_nput[g], 16 * NGROUP * i)
                    t0 = (i * NRING + g) * NGROUP
                    dve.tensor_copy(NR[:, g, :, D:ROW].bitcast(I32), meta[:, bass.ds(t0, NGROUP), :])
                    dve.tensor_copy(NX[:, g, :], rank[:, bass.ds(t0, NGROUP)]).then_inc(s_nmeta, 1)
            dve.wait_ge(s_order, 1)
            with dve.If(order_unknown(mybir.EngineType.DVE)):
                dve.wait_ge(s_metaready, 1)
                turns(dve, NIT, fill_meta)

            dve.wait_ge(s_w2, 1)
            link(dve.tensor_copy(w2t[:, :], PS[:, 7, 0:P]))
            dve.wait_ge(s_w, 16 * 8)
            link(dve.tensor_copy(fcx[:, 0:D], fcw[:, :]))
            for n, row in enumerate((al_row, ar_row)):
                link(dve.tensor_tensor(fca[:, n, :], fcw[:, :], row[:, :], ALU.mult))
                link(dve.tensor_reduce(fcx[:, D + n * HEADS:D + (n + 1) * HEADS],
                                       fca[:, n, :].rearrange("p (h f) -> p h f", h=HEADS), AX_X, ALU.add))
            link(dve.memset(acc[:, :, :], 0.0))
            link(dve.memset(elmax[:, :, :], -3.0e38))
            dve.wait_ge(s_tbl, 64)
            dve.wait_ge(s_x, 32)

            DVE = mybir.EngineType.DVE

            def after_tile_before(p, i, q, j):
                if used(i, q, 1) or j > 0:
                    dve.wait_ge(p.added, GROUP * group(i, q) + j)

            def onehots_a(i, q):
                g, n = q % SIDES, group(i, q)
                Ri = R[:, g, :, :].bitcast(I32)
                dve.wait_ge(a.load[g], 32 * GROUP * (use(i, q, SIDES) + 1))
                dve.tensor_tensor(DL[:, g, :], Ri[:, :, DST], node0[:, bass.ds(GROUP * n, GROUP)],
                                  ALU.subtract).then_inc(s_dl, 1)
                dve.tensor_copy(src_of[:, bass.ds(GROUP * n, GROUP)], Ri[:, :, SRC])
                freed(dve, a.summed, i, q, SIDES)
                dve.wait_ge(s_dl, n + 1)
                for j in range(GROUP):
                    t = dve.tensor_scalar(OH[:, g, j, :], iota[:, :], DL[:, g, j:j + 1], None, ALU.is_equal)
                t.then_inc(a.onehot, 1)
                dve.tensor_copy(dloc[:, bass.ds(GROUP * n, GROUP)], DL[:, g, :])
                dve.tensor_scalar(inside[:, g, :], DL[:, g, :], 0.0, None, ALU.is_ge).then_inc(s_in, 1)
                dve.wait_ge(s_in, 2 * n + 1)
                dve.scalar_tensor_tensor(outside[:, g, :], DL[:, g, :], float(P), inside[:, g, :],
                                         ALU.is_ge, ALU.subtract).then_inc(s_in, 1)

            def layer0(i, q):
                g, n = q % SIDES, group(i, q)
                Ri = R[:, g, :, :].bitcast(I32)
                dve.wait_ge(a.gather[q % DEEP], 16 * GROUP * (use(i, q, DEEP) + 1))
                dve.tensor_tensor(M1[:, g, :, :], G[:, q % DEEP, :, 0:D], R[:, g, :, 0:D], ALU.mult).then_inc(a.scaled, 1)
                if used(i, q, SIDES):
                    dve.wait_ge(a.put[g], 16 * GROUP * use(i, q, SIDES))
                dve.tensor_copy(M[:, g, :, D:ROW2].bitcast(I32), Ri[:, :, SRC_IN_BLOCK:SRC_IN_BLOCK + 1])
                dve.wait_ge(s_in, 2 * n + 2)
                dve.scalar_tensor_tensor(IX[:, g, :], outside[:, g, :], float(SLOTS), Ri[:, :, SRC_SLOT], ALU.mult, ALU.add)
                dve.wait_ge(a.looked, n + 1)
                dve.tensor_tensor(M[:, g, :, 0:D], PS[:, 2 + g, :].rearrange("p (j f) -> p j f", f=D),
                                  R[:, g, :, 0:D], ALU.mult).then_inc(s_m2, 1)
                regs = columns(DVE, columns_of[0], n)
                dve.wait_ge(a.summed, n + 1)
                for j in range(GROUP):
                    at = acc_flat[:, bass.ds(regs[j], D)]
                    after_tile_before(a, i, q, j)
                    dve.tensor_tensor(at, PS[:, 4 + g, j * P:(j + 1) * P], at, ALU.add).then_inc(a.added, 1)
            pipeline(dve, (onehots_a, 0), (layer0, 0))

            def onehots_c(i, q):
                d = q % DEEP
                dve.wait_ge(c.load[d], 16 * (use(i, q, DEEP) + 1))
                freed(dve, c.summed, i, q, DEEP)
                for j in range(GROUP):
                    t = dve.tensor_scalar(OHF[:, d, j, :], iota[:, :], S[:, d, j, D:D + 1].bitcast(I32),
                                          None, ALU.is_equal)
                t.then_inc(c.onehot, 1)
            pipeline(dve, (onehots_c, 0))
            dve.wait_ge(a.added, TILES)
            link(dve.tensor_tensor(X[:, :], X[:, :], acc_flat, ALU.add))
            nroot = [0]

            def bank(ap, blocks):
                return ap[:, blocks[0] * D:(blocks[-1] + 1) * D]

            def measure(blocks):
                for b in blocks:
                    end = dve.bn_stats(stats[:, b, :], X3[:, b, :])
                link(end)

            def norm():
                for b in range(NB):
                    end = dve.bn_aggr(meanvar[:, b, :], stats[:, b, :])
                link(end)
                nroot[0] += 1
                dve.tensor_scalar(nvar[:, :], meanvar[:, :, 1], EPS, None, ALU.add).then_inc(s_var, 1)
                dve.wait_ge(s_std, nroot[0])
                link(dve.reciprocal(rstd[:, :], nvar[:, :]))
                for b in range(NB):
                    end = dve.tensor_scalar(X3[:, b, :], X3[:, b, :], meanvar[:, b, 0:1], rstd[:, b:b + 1],
                                             ALU.subtract, ALU.mult)
                link(end)

            dve.wait_ge(c.summed, GROUPS)
            for blocks in BANKS:
                link(dve.tensor_tensor(bank(X, blocks), bank(X, blocks), bank(SUMS, blocks), ALU.add))
                measure(blocks)
            norm()
            dve.sem_inc(s_nx, 1)

            for t, blocks in enumerate(TRIOS):
                n, b = len(blocks), blocks[0]
                dve.wait_ge(s_nh, t + 1)
                dve.tensor_copy(erm[:, b:b + n, 0:HEADS],
                                PS[:, 2 + t % 2, 0:n * HW].rearrange("p (b c) -> p b c", c=HW)[:, :, ROW:HW]).then_inc(s_ne, 1)
            dve.wait_ge(s_ne, len(TRIOS))

            def three_parts(whole, part):
                n = whole.shape[2]
                spare = rest[:, :, 0:n]
                link(dve.tensor_copy(part(0), whole))
                link(dve.tensor_tensor(spare, whole, part(0), ALU.subtract))
                link(dve.tensor_copy(part(1), spare))
                link(dve.tensor_tensor(spare, spare, part(1), ALU.subtract))
                link(dve.tensor_copy(part(2), spare))

            HLB = HL[:, :, ROW:WIDE].bitcast(BF16)
            three_parts(HL[:, :, D:ROW], lambda k: HLB[:, :, k * HEADS:(k + 1) * HEADS])
            dve.sem_inc(s_tab[0], 1)
            link(dve.tensor_tensor(acc[:, :, :], X3, b1_row[:, :].unsqueeze(1).to_broadcast([P, NB, D]), ALU.add))
            link(dve.tensor_tensor(acc[:, :, :], acc[:, :, :], X3, ALU.add))

            def not_member(i, q, j):
                g, n = q % SIDES, group(i, q)
                t = dve.tensor_scalar(NOT[:, g, j, :], iota_b[:, :], dloc[:, bass.ds(GROUP * n + j, 1)],
                                      -1.0, ALU.is_equal, ALU.add)
                if j == GROUP - 1:
                    t.then_inc(m.onehot, 1)

            def maxima(i, q):
                g, n = q % SIDES, group(i, q)
                later = (i + (q + 2) // TURN, (q + 2) % TURN)
                regs = columns(DVE, columns_of[0], n, MAXIMUM)
                for k in range(2):
                    dve.wait_ge(m.summed, GROUP * n + 2 * k + 2)
                    dve.tensor_reduce(tmax[:, g, 2 * k:2 * k + 2, :],
                                      PS[:, 2 * k:2 * k + 2, :].rearrange("p j (h e) -> p j h e", h=HEADS),
                                      AX_X, ALU.max).then_inc(s_mx, 1)
                dve.wait_ge(s_mx, 2 * n + 2)
                for j in range(GROUP):
                    at = elmax_flat[:, bass.ds(regs[j], HEADS)]
                    after_tile_before(m, i, q, j)
                    dve.tensor_tensor(at, tmax[:, g, j, :], at, ALU.max).then_inc(m.added, 1)
                    if not isinstance(later[0], int) or later[0] < IT:
                        not_member(*later, j)
            for q in range(SIDES):
                for j in range(GROUP):
                    not_member(0, q, j)
            pipeline(dve, (maxima, 0))
            dve.wait_ge(m.added, TILES)
            link(dve.tensor_scalar(elmax[:, :, :], elmax[:, :, :], -1.0e30, None, ALU.max))
            link(dve.tensor_tensor(small[:, :, :], elmax[:, :, :], erm[:, :, 0:HEADS], ALU.add))
            link(dve.tensor_scalar(elmax[:, :, :], small[:, :, :], SLOPE, None, ALU.mult))
            link(dve.tensor_tensor(erm[:, :, HEADS:2 * HEADS], elmax[:, :, :], small[:, :, :], ALU.max))
            three_parts(erm[:, :, :], lambda k: erm_b[:, :, k, :])
            dve.sem_inc(s_tab[0], 1)

            def onehots_w(i, q):
                n, d = group(i, q), q % DEEP
                freed(dve, w.summed, i, q, DEEP)
                for j in range(GROUP):
                    t = dve.tensor_scalar(OHB[:, d, j, :], iota_b[:, :], dloc[:, bass.ds(GROUP * n + j, 1)],
                                          None, ALU.is_equal)
                t.then_inc(w.onehot, 1)

            def logits(i, q):
                g, d, n = q % SIDES, q % DEEP, group(i, q)

                def flat(ap):
                    return ap[:, g, :, :].rearrange("p j h -> p (j h)")
                dve.wait_ge(w.load[d], 16 * (use(i, q, DEEP) + 1))
                dve.wait_ge(s_lc, n + 1)
                dve.tensor_tensor(logit[:, g, :, :], looked[:, d, :, 0:HEADS], S[:, d, :, D:ROW], ALU.add).then_inc(s_lg, 1)
                dve.wait_ge(s_lg, n + 1)
                dve.scalar_tensor_tensor(flat(slope), flat(logit), SLOPE, flat(logit), ALU.mult, ALU.max).then_inc(s_lk, 1)
                dve.wait_ge(s_lk, n + 1)
                dve.tensor_tensor(logit[:, g, :, :], slope[:, g, :, :], looked[:, d, :, HEADS:2 * HEADS],
                                  ALU.subtract).then_inc(s_lg2, 1)
                dve.wait_ge(s_lg2, n + 1)
                freed(dve, s_ex, i, q, SIDES)
                dve.tensor_scalar(shift[:, g, :, :], logit[:, g, :, :], 0.0, None, ALU.min).then_inc(s_sh, 1)

            def messages(i, q):
                d, n = q % DEEP, group(i, q)
                dve.wait_ge(s_ex, n + 1)
                rows = S[:, d, :, 0:D].rearrange("p j (h f) -> p j h f", h=HEADS)
                dve.tensor_tensor(rows, rows, prob[:, d, :, :].unsqueeze(3).to_broadcast([P, GROUP, HEADS, HF]),
                                  ALU.mult).then_inc(w.scaled, 1)

            def take_looked(i, q):
                dve.wait_ge(w.looked, group(i, q) + 1)
                dve.tensor_reduce(looked[:, q % DEEP, :, :], LOOKED.rearrange("p j (k c) -> p j c k", k=3),
                                  AX_X, ALU.add).then_inc(s_lc, 1)
            pipeline(dve, (logits, 1), (onehots_w, 3), (messages, 1), (take_looked, 2))
            dve.wait_ge(w.summed, GROUPS)
            link(dve.tensor_copy(acc1[:, :, :].rearrange("p b f -> p (b f)"), WSUMS))
            for k in (1, 2):
                link(dve.tensor_tensor(acc1[:, :, 0:HEADS], acc1[:, :, 0:HEADS], acc1[:, :, k * HEADS:(k + 1) * HEADS],
                                       ALU.add))
            link(dve.tensor_scalar(small[:, :, :], acc1[:, :, 0:HEADS], 1e-20, None, ALU.max))
            link(dve.reciprocal(elmax[:, :, :], small[:, :, :]))
            for blocks in BANKS:
                n, b = len(blocks), blocks[0]
                link(dve.tensor_tensor(bank(Yf, blocks).rearrange("p (h f) -> p h f", f=HF),
                                       bank(SUMS, blocks).rearrange("p (h f) -> p h f", f=HF),
                                       elmax_flat[:, b * HEADS:(b + n) * HEADS].unsqueeze(2).to_broadcast([P, n * HEADS, HF]),
                                       ALU.mult))
                link(dve.tensor_tensor(bank(X, blocks), bank(Yf, blocks), bank(acc_flat, blocks), ALU.add))
                measure(blocks)
            dve.sem_inc(s_tot_w, 1)
            nroot[0] += 1
            dve.tensor_scalar(dinv[:, :], acc1[:, :, LW - 1], 1.0, None, ALU.add).then_inc(s_var, 1)
            dve.wait_ge(s_std, nroot[0])
            link(dve.reciprocal(dinv[:, :], dinv[:, :]))
            norm()
            dve.sem_inc(s_tab[1], 1)

            def onehots_of(p):
                def step(i, q):
                    n, d = group(i, q), q % DEEP
                    freed(dve, p.summed, i, q, DEEP)
                    for j in range(GROUP):
                        t = dve.tensor_scalar(OHF[:, d, j, :], iota[:, :], dloc[:, bass.ds(GROUP * n + j, 1)],
                                              None, ALU.is_equal)
                    t.then_inc(p.onehot, 1)
                pipeline(dve, (step, 0))

            link(dve.tensor_tensor(Y[:, :, :], X3, b2_row[:, :].unsqueeze(1).to_broadcast([P, NB, D]), ALU.add))
            onehots_of(l2)
            for k, blocks in enumerate(BANKS):
                dve.wait_ge(s_p2, k + 1)
                if k == 0:
                    dve.wait_ge(s_tabw[1], 16)
                link(dve.tensor_tensor(bank(X, blocks), bank(Yf, blocks), bank(SUMS, blocks), ALU.add))
                measure(blocks)
            norm()
            for b in range(NB):
                end = dve.tensor_scalar(Y[:, b, :], X3[:, b, :], dinv[:, b:b + 1], None, ALU.mult)
            link(end)
            dve.sem_inc(s_tot_2, 1)
            dve.sem_inc(s_tab[2], 1)

            onehots_of(l3)
            for k, blocks in enumerate(BANKS):
                dve.wait_ge(s_p3, k + 1)
                if k == 0:
                    dve.wait_ge(s_tabw[2], 16)
                for b in blocks:
                    end = dve.scalar_tensor_tensor(Y[:, b, :], SUMS[:, b * D:(b + 1) * D], dinv[:, b:b + 1], b3_row[:, :],
                                                    ALU.mult, ALU.add)
                link(end)
                link(dve.scalar_tensor_tensor(bank(X, blocks), bank(Yf, blocks), 0.0, bank(X, blocks), ALU.max, ALU.add))
                measure(blocks)
            norm()
            dve.sem_inc(s_fin, 1)


_INS = ['x', 'src', 'dst', 'edge_attr_128', 'L1_gnn_fc_w', 'L1_gnn_attn_l', 'L1_gnn_attn_r', 'L1_gnn_bias',
        'L2_gnn_W', 'L2_gnn_b', 'L3_gnn_W', 'L3_gnn_b']
_OUTS = [((3125, 128), 'float32')]


def kernel(**inputs):
    import numpy as _np
    import concourse.bacc as _bacc
    from concourse import mybir as _mybir
    from concourse.bass_utils import run_bass_kernel_spmd as _run

    nc = _bacc.Bacc("TRN2", target_bir_lowering=False, num_devices=1)
    arrays, args = {}, []
    for name in _INS:
        a = _np.ascontiguousarray(inputs[name])
        arrays[f"in_{name}_dram"] = a
        args.append(nc.dram_tensor(f"in_{name}_dram", a.shape, _mybir.dt.from_np(a.dtype), kind="ExternalInput").ap())
    for i, (shape, dtype) in enumerate(_OUTS):
        dt = _mybir.dt.from_np(_np.dtype(dtype))
        args.append(nc.dram_tensor(f"out_{i}_dram", shape, dt, kind="ExternalOutput").ap())
    gnn_program(nc, *args)
    r = _run(nc, [arrays], core_ids=[0])
    got = tuple(r.results[0][f"out_{i}_dram"] for i in range(len(_OUTS)))
    return got[0]
```
